# Optimizing a Trainium2 kernel written in Bass

```python
import numpy as np
import jax
import jax.numpy as jnp

def _softmax(x, axis=-1):
    return jax.nn.softmax(x, axis=axis)

def _gelu(x):
    return jax.nn.gelu(x, approximate=True)

def _silu(x):
    return jax.nn.silu(x)

def _sigmoid(x):
    return jax.nn.sigmoid(x)

def _layernorm(x, axis=-1, eps=1e-05):
    m = jnp.mean(x, axis=axis, keepdims=True)
    v = jnp.var(x, axis=axis, keepdims=True)
    return (x - m) / jnp.sqrt(v + eps)

def _scatter_add(tgt, idx, src, axis=0):
    return tgt.at[idx].add(src)

def _segment_sum(src, seg, n):
    return jax.ops.segment_sum(src, seg, n)
kernel_name = 'mk_xattn_ffn_d1_seqx_r8_a19e84'

def setup_inputs(seed: int=0):
    np.random.seed(seed)
    _w = jnp.asarray

    def _rec_inputs():
        import jax
        import jax.numpy as jnp
        _rk = jax.random.key(seed)
        x = -0.0002928 + 1 * jax.random.normal(jax.random.fold_in(_rk, 1), (4, 512, 128), jnp.float32)
        _lenS = 512 - jax.random.randint(jax.random.fold_in(_rk, 7), (4,), 0, max(1, 512 // 4) + 1, jnp.int32)
        _lenS2 = 32 - jax.random.randint(jax.random.fold_in(_rk, 8), (4,), 0, max(1, 32 // 4) + 1, jnp.int32)
        _ctx_1024P = jax.random.normal(jax.random.fold_in(_rk, 11), (4, 16, 128), jnp.float32)
        _ctx_1024c = jax.random.dirichlet(jax.random.fold_in(_rk, 511), 0.3 * jnp.ones((16,), jnp.float32), (4, 32))
        _ctx_1024t = jnp.einsum('bsk,bkd->bsd', _ctx_1024c, _ctx_1024P)
        _ctx_1024t = _ctx_1024t * jax.lax.rsqrt(jnp.mean(jnp.square(_ctx_1024t)) + 1e-12) * 0.953939
        ctx_1024 = -1.39393e-06 + 0.999914 * (_ctx_1024t + 0.3 * jax.random.normal(jax.random.fold_in(_rk, 611), (4, 32, 128), jnp.float32))
        _validS = jnp.arange(512)[None, :] < _lenS[:, None]
        _validS2 = jnp.arange(32)[None, :] < _lenS2[:, None]
        _causal = jnp.tril(jnp.ones((512, 512), dtype=bool))
        mask_Bx1xSxS2_ff0 = jnp.where(jnp.ones((4, 1, 512, 32), dtype=bool), 0.0, -1000000000.0).astype(jnp.float32)
        return (x, ctx_1024, mask_Bx1xSxS2_ff0)
    x, ctx_1024, mask_Bx1xSxS2_ff0 = _rec_inputs()

    def _L0_xattn_setup():
        import jax, jax.numpy as jnp
        import numpy as np
        B, S, D, H = (2, 256, 128, 16)
        HD = D // H

        def _split_heads(x):
            b, s, _ = x.shape
            return x.reshape(b, s, H, HD).transpose(0, 2, 1, 3)
        key = jax.random.key(seed)
        ks = jax.random.split(key, 12)
        init = lambda k, shape: jax.random.normal(k, shape, dtype=jnp.float32) * (1.0 / np.sqrt(shape[0]))
        return {'q': jax.random.normal(ks[0], (B, S, D), dtype=jnp.float32), 'k': jax.random.normal(ks[1], (B, S, D), dtype=jnp.float32), 'v': jax.random.normal(ks[2], (B, S, D), dtype=jnp.float32), 'mask': jnp.zeros((B, 1, S, S), dtype=jnp.float32), 'Wq': init(ks[3], (D, D)), 'bq': jnp.zeros((D,), jnp.float32), 'Wk': init(ks[4], (D, D)), 'bk': jnp.zeros((D,), jnp.float32), 'Wv': init(ks[5], (D, D)), 'bv': jnp.zeros((D,), jnp.float32), 'Wo': init(ks[6], (D, D)), 'bo': jnp.zeros((D,), jnp.float32)}
    _L0_xattn_all = _L0_xattn_setup()
    _L0_xattn_in = {k: v for k, v in _L0_xattn_all.items() if k in ('Wq', 'bq', 'Wk', 'bk', 'Wv', 'bv', 'Wo', 'bo')}
    del _L0_xattn_all

    def _L0_ffn_setup():
        import jax, jax.numpy as jnp
        import numpy as np
        QMAX = 127.0

        def _quant_dequant(w):
            scale = jnp.max(jnp.abs(w), axis=-1, keepdims=True) / QMAX
            scale = jnp.maximum(scale, 1e-08)
            q = jnp.clip(jnp.round(w / scale), -QMAX, QMAX)
            return q * scale
        key = jax.random.key(seed)
        ks = jax.random.split(key, 7)
        B, S, D, F, E, NS = (2, 256, 128, 256, 8, 1)
        std = 1.0 / np.sqrt(D)
        x = jax.random.normal(ks[0], (B, S, D), dtype=jnp.float32)
        router_w = _quant_dequant(jax.random.normal(ks[1], (E, D), dtype=jnp.float32) * std)
        router_b = jnp.zeros((E,), dtype=jnp.float32)
        w_up = _quant_dequant(jax.random.normal(ks[2], (E, F, D), dtype=jnp.float32) * std)
        w_down = _quant_dequant(jax.random.normal(ks[3], (E, D, F), dtype=jnp.float32) / np.sqrt(F))
        shared_w_up = _quant_dequant(jax.random.normal(ks[4], (NS, F, D), dtype=jnp.float32) * std)
        shared_w_down = _quant_dequant(jax.random.normal(ks[5], (NS, D, F), dtype=jnp.float32) / np.sqrt(F))
        return {'x': x, 'router_w': router_w, 'router_b': router_b, 'w_up': w_up, 'w_down': w_down, 'shared_w_up': shared_w_up, 'shared_w_down': shared_w_down}
    _L0_ffn_all = _L0_ffn_setup()
    _L0_ffn_in = {k: v for k, v in _L0_ffn_all.items() if k in ('router_w', 'router_b', 'w_up', 'w_down', 'shared_w_up', 'shared_w_down')}
    del _L0_ffn_all
    return {'x': x, 'ctx_1024': ctx_1024, 'mask_Bx1xSxS2_ff0': mask_Bx1xSxS2_ff0, 'L0_xattn_Wq': _L0_xattn_in['Wq'], 'L0_xattn_bq': _L0_xattn_in['bq'], 'L0_xattn_Wk': _L0_xattn_in['Wk'], 'L0_xattn_bk': _L0_xattn_in['bk'], 'L0_xattn_Wv': _L0_xattn_in['Wv'], 'L0_xattn_bv': _L0_xattn_in['bv'], 'L0_xattn_Wo': _L0_xattn_in['Wo'], 'L0_xattn_bo': _L0_xattn_in['bo'], 'L0_ffn_router_w': _L0_ffn_in['router_w'], 'L0_ffn_router_b': _L0_ffn_in['router_b'], 'L0_ffn_w_up': _L0_ffn_in['w_up'], 'L0_ffn_w_down': _L0_ffn_in['w_down'], 'L0_ffn_shared_w_up': _L0_ffn_in['shared_w_up'], 'L0_ffn_shared_w_down': _L0_ffn_in['shared_w_down']}

def reference(x, ctx_1024, mask_Bx1xSxS2_ff0, L0_xattn_Wq, L0_xattn_bq, L0_xattn_Wk, L0_xattn_bk, L0_xattn_Wv, L0_xattn_bv, L0_xattn_Wo, L0_xattn_bo, L0_ffn_router_w, L0_ffn_router_b, L0_ffn_w_up, L0_ffn_w_down, L0_ffn_shared_w_up, L0_ffn_shared_w_down):
    import jax
    import jax.numpy as jnp

    def _L0_xattn_ref(q, k, v, mask, Wq, bq, Wk, bk, Wv, bv, Wo, bo):
        import jax, jax.numpy as jnp
        import numpy as np
        B, S, D, H = (2, 256, 128, 16)
        HD = D // H

        def _split_heads(x):
            b, s, _ = x.shape
            return x.reshape(b, s, H, HD).transpose(0, 2, 1, 3)
        qh = _split_heads(q @ Wq + bq)
        kh = _split_heads(k @ Wk + bk)
        vh = _split_heads(v @ Wv + bv)
        scores = jnp.einsum('bhqd,bhkd->bhqk', qh, kh) / jnp.sqrt(jnp.float32(D))
        scores = scores + mask * -1000000000.0
        attn = jax.nn.softmax(scores, axis=-1)
        out = jnp.einsum('bhqk,bhkd->bhqd', attn, vh)
        out = out.transpose(0, 2, 1, 3).reshape(q.shape[0], -1, D)
        return out @ Wo + bo

    def _L0_ffn_ref(x, router_w, router_b, w_up, w_down, shared_w_up, shared_w_down):
        import jax, jax.numpy as jnp
        import numpy as np
        QMAX = 127.0

        def _quant_dequant(w):
            scale = jnp.max(jnp.abs(w), axis=-1, keepdims=True) / QMAX
            scale = jnp.maximum(scale, 1e-08)
            q = jnp.clip(jnp.round(w / scale), -QMAX, QMAX)
            return q * scale
        B, S, D = x.shape
        E = router_w.shape[0]
        TOPK = 2
        xt = x.reshape(-1, D)
        logits = xt @ router_w.T + router_b
        probs = jax.nn.softmax(logits, axis=-1)
        top_vals, top_idx = jax.lax.top_k(probs, TOPK)
        top_vals = top_vals / jnp.sum(top_vals, axis=-1, keepdims=True)
        combine = jnp.sum(jax.nn.one_hot(top_idx, E, dtype=xt.dtype) * top_vals[..., None], axis=1)
        h = jnp.einsum('td,efd->tef', xt, w_up)
        y = jnp.einsum('tef,edf->ted', jax.nn.silu(h), w_down)
        out = jnp.einsum('ted,te->td', y, combine)
        hs = jnp.einsum('td,sfd->tsf', xt, shared_w_up)
        out = out + jnp.einsum('tsf,sdf->td', jax.nn.silu(hs), shared_w_down)
        return out.reshape(B, S, D)
    x = x + _L0_xattn_ref(_layernorm(x, axis=-1), ctx_1024, ctx_1024, mask_Bx1xSxS2_ff0, L0_xattn_Wq, L0_xattn_bq, L0_xattn_Wk, L0_xattn_bk, L0_xattn_Wv, L0_xattn_bv, L0_xattn_Wo, L0_xattn_bo)
    x = x + _L0_ffn_ref(_layernorm(x, axis=-1), L0_ffn_router_w, L0_ffn_router_b, L0_ffn_w_up, L0_ffn_w_down, L0_ffn_shared_w_up, L0_ffn_shared_w_down)
    return x

_drawn_inputs = setup_inputs


def setup_inputs(seed=0):
    import zlib

    import numpy as np

    out = dict(_drawn_inputs(seed))
    spreads = {'L0_xattn_bq': (0.0, 0.405),
     'L0_xattn_bk': (0.0, 0.8),
     'L0_xattn_bv': (0.0, 0.1),
     'L0_xattn_bo': (0.0, 0.1),
     'L0_ffn_router_b': (0.0, 0.1)}
    factors = {}
    for name, (base, spread) in spreads.items():
        noise = np.random.default_rng([zlib.crc32(name.encode()), seed]).standard_normal(out[name].shape)
        drawn = base * np.exp(spread * noise) if base else spread * noise
        out[name] = jnp.asarray(drawn.astype(out[name].dtype))
    for name, factor in factors.items():
        out[name] = (out[name] * factor).astype(out[name].dtype)
    return out
```

```python
from contextlib import ExitStack

import numpy as np

import concourse.bass as bass
from concourse import mybir

F32 = mybir.dt.float32
F32R = mybir.dt.float32r
BF16 = mybir.dt.bfloat16
U32 = mybir.dt.uint32
ALU = mybir.AluOpType
ACT = mybir.ActivationFunctionType
AX_X = mybir.AxisListType.X

P = 128
B, S, D = 4, 512, 128
CTX = 32
H, HD = 16, 8
GH = P // CTX
NG = H // GH
NT = S // P
E, F = 8, 256
NE = E + 1
FC = F // P
NU = NE * FC
TOPK = 2
PARTS = 3
SCALE = 1.0 / float(np.sqrt(np.float32(D)))
MASK_SCALE = -1000000000.0
LN_EPS = 1e-5

C_IDENT = 0
C_HEAD = C_IDENT + P
C_GROUP = C_HEAD + H
C_ONES = C_GROUP + GH
C_IOTA = C_ONES + CTX
C_PICK = C_IOTA + E
C_END = C_PICK + E * P


def shape_constants():
    c = np.zeros((P, C_END), np.float32)
    p = np.arange(P)
    c[:, C_IDENT:C_HEAD] = np.eye(P, dtype=np.float32)
    c[:, C_HEAD:C_GROUP] = p[:, None] // HD == np.arange(H)[None, :]
    c[:, C_GROUP:C_ONES] = p[:, None] // CTX == np.arange(GH)[None, :]
    c[:, C_ONES:C_IOTA] = p[:, None] // CTX == np.arange(CTX)[None, :] // HD
    c[:, C_IOTA:C_PICK] = np.arange(E)[None, :]
    rows = np.arange(PARTS * E)
    pick = rows[:, None] % E == np.arange(E)[None, :]
    c[: PARTS * E, C_PICK:] = np.repeat(pick, P, axis=1)
    return c


def xattn_moe(nc: bass.Bass, x, ctx_t, mask, wq, bq, wk, bk, wv, bv, wo, bo,
              router_t, router_b, w_up_t, w_down_t, consts, out):
    with ExitStack() as stack:
        def sb(name, shape, dt=F32):
            return stack.enter_context(nc.sbuf_tensor(name, shape, dt))

        def bank(name):
            return stack.enter_context(nc.psum_tensor(name, [P, S], F32))

        def sem(name):
            return stack.enter_context(nc.semaphore(name))

        cst = sb("cst", [P, C_END])
        ident = cst[:, C_IDENT:C_HEAD]
        pick = sb("pick", [PARTS * E, E * P], BF16)
        ident16 = sb("ident16", [P, P], BF16)
        xin = sb("xin", [P, B, NT, D])
        msk = sb("msk", [P, B, NT, CTX])
        ctxt = sb("ctxt", [D, B * CTX])
        ctxrep = sb("ctxrep", [D, B, GH, CTX])
        wq_s, wk_s, wv_s, wo_s = sb("wq_s", [D, D]), sb("wk_s", [D, D]), sb("wv_s", [D, D]), sb("wo_s", [D, D])
        bq_s, bk_s = sb("bq_s", [D, 1]), sb("bk_s", [D, 1])
        bv_s, bo_s, rb_s = sb("bv_s", [P, D]), sb("bo_s", [P, D]), sb("rb_s", [P, E])
        rt = sb("rt", [D, E])
        rt_hi, rt_lo = sb("rt_hi", [D, E], F32R), sb("rt_lo", [D, E], F32R)
        wup = sb("wup", [D, NE * F])
        wup_hi, wup_lo = sb("wup_hi", [D, NE * F], F32R), sb("wup_lo", [D, NE * F], F32R)
        wdn = sb("wdn", [P, NU, D])
        kt = sb("kt", [D, B * CTX])
        kblk = sb("kblk", [D, B, H, CTX])
        kblk_hi, kblk_lo = sb("kblk_hi", [D, B, H * CTX], F32R), sb("kblk_lo", [D, B, H * CTX], F32R)
        vrep = sb("vrep", [P, B, D])
        vblk = sb("vblk", [P, B, D])
        eps = sb("eps", [P, 2 * NT])
        stats = sb("stats", [P, NT, 6])
        mv = sb("mv", [P, 2, NT, 2])
        vareps = sb("vareps", [P, NT])
        rstd = sb("rstd", [P, 2, NT])
        xn = sb("xn", [P, NT, D])
        xnt = sb("xnt", [D, S])
        qt_hi, qt_lo = sb("qt_hi", [D, S], F32R), sb("qt_lo", [D, S], F32R)
        score = sb("score", [P, NT, H, CTX])
        rowmax = sb("rowmax", [P, NT, H])
        prob = sb("prob", [P, NT, H * CTX])
        probt = sb("probt", [P, NG, S])
        rsum = sb("rsum", [D, S])
        ot = sb("ot", [D, S])
        xb = sb("xb", [P, B, NT, D])
        x2 = sb("x2", [P, B, NT, D])
        xn2 = sb("xn2", [P, NT, D])
        x2t_hi, x2t_lo = sb("x2t_hi", [D, S], F32R), sb("x2t_lo", [D, S], F32R)
        logit = sb("logit", [P, NT, E])
        top = sb("top", [P, NT, 8])
        topi = sb("topi", [P, NT, 8], U32)
        lead = sb("lead", [P, NT])
        tanh = sb("tanh", [P, NT])
        topw = sb("topw", [P, NT, TOPK])
        hot = sb("hot", [P, TOPK, NT, E])
        comb = sb("comb", [P, NT, E])
        rest1, rest2 = sb("rest1", [P, NT, E]), sb("rest2", [P, NT, E])
        parts = sb("parts", [P, NT, PARTS, E], BF16)
        combt = sb("combt", [PARTS * E, S], BF16)
        silu = sb("silu", [P, 4, S])
        act_in = sb("act_in", [P, 4, S])
        yt = sb("yt", [D, S])
        res = sb("res", [P, B, NT, D])

        hid = [bank("hid0"), bank("hid1")]
        yacc = bank("yacc")
        cbc = bank("cbc")
        sc = bank("sc")
        tp = bank("tp")
        pv = bank("pv")
        mx = bank("mx")

        in_x = [sem(f"in_x{b}") for b in range(B)]
        in_ctx, in_cst, in_wq, in_kv, in_mask = sem("in_ctx"), sem("in_cst"), sem("in_wq"), sem("in_kv"), sem("in_mask")
        in_bias, in_wo, in_router, in_up, in_down = sem("in_bias"), sem("in_wo"), sem("in_router"), sem("in_up"), sem("in_down")
        out_stored = sem("out_stored")
        k_done, v_done = sem("k_done"), sem("v_done")
        xt_done, q_done, s_done, ptr_done, pv_done = sem("xt_done"), sem("q_done"), sem("s_done"), sem("ptr_done"), sem("pv_done")
        wo_done, x2t_done, logit_done, ct_done, cbc_done = sem("wo_done"), sem("x2t_done"), sem("logit_done"), sem("ct_done"), sem("cbc_done")
        up_done, down_done, outt_done = sem("up_done"), sem("down_done"), sem("outt_done")
        upw_hi, xnt_copied, qhi_ready, prob_ready, pt_copied = sem("upw_hi"), sem("xnt_copied"), sem("qhi_ready"), sem("prob_ready"), sem("pt_copied")
        x2hi_ready, tanh_ready, silu_ready, yt_ready = sem("x2hi_ready"), sem("tanh_ready"), sem("silu_ready"), sem("yt_ready")
        dve_step = sem("dve_step")
        kt_ready, kblk0_ready, vblk_ready, const_ready, upw_lo = sem("kt_ready"), sem("kblk0_ready"), sem("vblk_ready"), sem("const_ready"), sem("upw_lo")
        stats_ready, xn_ready, qlo_ready, max_ready, ot_ready = sem("stats_ready"), sem("xn_ready"), sem("qlo_ready"), sem("max_ready"), sem("ot_ready")
        score_evac = sem("score_evac")
        x2_ready, stats2_ready, xn2_ready, x2lo_ready = sem("x2_ready"), sem("stats2_ready"), sem("xn2_ready"), sem("x2lo_ready")
        logit_ready, lead_ready, parts_ready, combt_ready, scaled_ready = sem("logit_ready"), sem("lead_ready"), sem("parts_ready"), sem("combt_ready"), sem("scaled_ready")
        res_ready = sem("res_ready")
        pool_step = sem("pool_step")
        eps_ready, rstd_ready, rstd2_ready, shifted_ready, xb_ready, kblk_ready = sem("eps_ready"), sem("rstd_ready"), sem("rstd2_ready"), sem("shifted_ready"), sem("xb_ready"), sem("kblk_ready")

        def scaled_upto(n):
            return (n // NU) * (NU - FC) + n % NU - FC + 1

        block = stack.enter_context(nc.Block())

        @block.sync
        def _(sp):
            sp.dma_start(xin[:, 0], x[0].rearrange("(p j) d -> p j d", j=NT)).then_inc(in_x[0], 16)
            sp.dma_start(cst[:, :], consts).then_inc(in_cst, 16)
            sp.dma_start(wq_s[:, :], wq).then_inc(in_wq, 16)
            sp.dma_start(bq_s[:, :], bq.rearrange("(d a) -> d a", a=1)).then_inc(in_wq, 16)
            sp.dma_start(msk[:, :, :, :], mask.rearrange("b a (p j) k -> p (b a) j k", j=NT)).then_inc(in_mask, 16)
            sp.dma_start(wo_s[:, :], wo).then_inc(in_wo, 16)
            sp.dma_start(wup[:, :], w_up_t).then_inc(in_up, 16)
            sp.dma_start(wdn[:, :, :], w_down_t).then_inc(in_down, 16)
            for b in range(1, B):
                sp.dma_start(xin[:, b], x[b].rearrange("(p j) d -> p j d", j=NT)).then_inc(in_x[b], 16)
            for b in range(B):
                sp.wait_ge(res_ready, b + 1)
                sp.dma_start(out[b].rearrange("(p j) d -> p j d", j=NT), res[:, b]).then_inc(out_stored, 16)
            sp.wait_ge(out_stored, 16 * B)

        @block.gpsimd
        def _(pool):
            steps = [0]

            def own(ins):
                steps[0] += 1
                ins.then_inc(pool_step, 1)
                pool.wait_ge(pool_step, steps[0])

            def root(src, dst, done):
                own(nc.gpsimd.tensor_scalar(vareps[:, :], mv[:, src, :, 1], LN_EPS, None, ALU.add))
                nc.gpsimd.tensor_tensor(rstd[:, src, :], vareps[:, :], eps[:, 0:NT], ALU.pow).then_inc(done, 1)

            nc.gpsimd.memset(eps[:, :], -0.5).then_inc(eps_ready, 1)
            pool.wait_ge(eps_ready, 1)
            for w in range(B):
                pool.wait_ge(stats_ready, w + 1)
                root(0, 0, rstd_ready)
                if w == 0:
                    pool.wait_ge(in_bias, 16 * 3)
                pool.wait_ge(in_x[w], 16)
                nc.gpsimd.tensor_tensor(xb[:, w], xin[:, w], bo_s[:, :].unsqueeze(1).broadcast_to([P, NT, D]),
                                        ALU.add).then_inc(xb_ready, 1)
                if w + 1 < B:
                    pool.wait_ge(kt_ready, 1)
                    k_next = kt[:, (w + 1) * CTX:(w + 2) * CTX].unsqueeze(1).broadcast_to([D, H, CTX])
                    heads = cst[:, C_HEAD:C_GROUP].unsqueeze(2).broadcast_to([D, H, CTX])
                    own(nc.gpsimd.tensor_tensor(kblk[:, w + 1], k_next, heads, ALU.mult))
                    flat = kblk[:, w + 1].rearrange("p h k -> p (h k)")
                    own(nc.gpsimd.tensor_copy(kblk_hi[:, w + 1], flat))
                    nc.gpsimd.tensor_tensor(kblk_lo[:, w + 1], flat, kblk_hi[:, w + 1].bitcast(F32),
                                            ALU.subtract).then_inc(kblk_ready, 1)
                for j in range(NT):
                    pool.wait_ge(max_ready, NT * w + j + 1)
                    nc.gpsimd.tensor_tensor(score[:, j], score[:, j], rowmax[:, j].unsqueeze(2).broadcast_to([P, H, CTX]),
                                            ALU.subtract).then_inc(shifted_ready, 1)
                pool.wait_ge(stats2_ready, w + 1)
                root(1, 1, rstd2_ready)

        @block.scalar
        def _(act):
            act.dma_start(ctxt[:, :], ctx_t[:, :, 0, :]).then_inc(in_ctx, 16)
            act.dma_start(wk_s[:, :], wk).then_inc(in_kv, 16)
            act.dma_start(bk_s[:, :], bk.rearrange("(d a) -> d a", a=1)).then_inc(in_kv, 16)
            act.dma_start(wv_s[:, :], wv).then_inc(in_kv, 16)
            act.dma_start(ctxrep[:, :, :, :], ctx_t).then_inc(in_ctx, 16)
            act.dma_start(bv_s[:, :], bv.partition_broadcast(P)).then_inc(in_bias, 16)
            act.dma_start(bo_s[:, :], bo.partition_broadcast(P)).then_inc(in_bias, 16)
            act.dma_start(rb_s[:, :], router_b.partition_broadcast(P)).then_inc(in_bias, 16)
            act.dma_start(rt[:, :], router_t).then_inc(in_router, 16)

            def silu_chunk(n):
                act.wait_ge(up_done, n + 1)
                f = n % FC
                if n % NU < FC:
                    if n >= 4:
                        act.wait_ge(down_done, n - 3)
                    nc.scalar.activation(act_in[:, n % 4], hid[f][:, :], ACT.Silu).then_inc(silu_ready, 1)
                else:
                    if (n - 4) % NU >= FC and n >= 4:
                        act.wait_ge(scaled_ready, scaled_upto(n - 4))
                    nc.scalar.activation(silu[:, n % 4], hid[f][:, :], ACT.Silu).then_inc(silu_ready, 1)

            def attention(b, s):
                if s == 1:
                    act.wait_ge(xt_done, b + 1)
                    nc.scalar.activation(xnt[:, :], tp[:, :], ACT.Copy).then_inc(xnt_copied, 1)
                if s == 2:
                    act.wait_ge(q_done, b + 1)
                    nc.scalar.activation(qt_hi[:, :], mx[:, :], ACT.Identity, bias=bq_s[:, :]).then_inc(qhi_ready, 1)
                if s == 8:
                    act.wait_ge(shifted_ready, NT * (b + 1))
                    nc.scalar.activation(prob[:, :, :], score[:, :, :, :].rearrange("p j h k -> p j (h k)"),
                                         ACT.Exp).then_inc(prob_ready, 1)
                if 9 <= s < 9 + NT:
                    j = s - 9
                    act.wait_ge(ptr_done, NT * b + j + 1)
                    nc.scalar.activation(probt[:, :, j * P:(j + 1) * P], tp[:, :].rearrange("p (g t) -> p g t", g=NG),
                                         ACT.Copy).then_inc(pt_copied, 1)
                if s == 17:
                    act.wait_ge(x2t_done, b + 1)
                    nc.scalar.activation(x2t_hi[:, :], tp[:, :], ACT.Copy).then_inc(x2hi_ready, 1)

            act.wait_ge(in_up, 16)
            nc.scalar.activation(wup_hi[:, :], wup[:, :], ACT.Copy).then_inc(upw_hi, 1)
            for w in range(B + 1):
                f = w - 1
                if f >= 0:
                    for c in range(FC):
                        silu_chunk(NU * f + c)
                    act.wait_ge(lead_ready, w)
                    nc.scalar.activation(tanh[:, :], lead[:, :], ACT.Tanh, scale=0.5).then_inc(tanh_ready, 1)
                for s in range(NU):
                    if f >= 0 and s % 2 == 0 and s // 2 + 1 < NE:
                        for c in range(FC):
                            silu_chunk(NU * f + FC * (s // 2 + 1) + c)
                    if w < B:
                        attention(w, s)
                if f >= 0:
                    act.wait_ge(down_done, NU * w)
                    nc.scalar.activation(yt[:, :], yacc[:, :], ACT.Copy).then_inc(yt_ready, 1)

        @block.vector
        def _(dve):
            steps = [0]

            def own(ins):
                steps[0] += 1
                ins.then_inc(dve_step, 1)
                dve.wait_ge(dve_step, steps[0])

            def layernorm_stats(src, which, done):
                for j in range(NT):
                    last = nc.vector.bn_stats(stats[:, j, :], src[:, j, :])
                own(last)
                for j in range(NT):
                    last = nc.vector.bn_aggr(mv[:, which, j, :], stats[:, j, :])
                last.then_inc(done, 1)

            def layernorm_apply(dst, src, which, done):
                for j in range(NT):
                    last = nc.vector.tensor_scalar(dst[:, j, :], src[:, j, :], mv[:, which, j, 0:1], rstd[:, which, j:j + 1],
                                                   ALU.subtract, ALU.mult)
                last.then_inc(done, 1)

            def setup_keys():
                dve.wait_ge(in_cst, 16)
                nc.vector.tensor_copy(pick[:, :], cst[0:PARTS * E, C_PICK:C_END])
                nc.vector.tensor_copy(ident16[:, :], ident).then_inc(const_ready, 1)
                dve.wait_ge(k_done, 1)
                nc.vector.tensor_scalar(kt[:, :], mx[:, 0:B * CTX], bk_s[:, :], SCALE, ALU.add, ALU.mult).then_inc(kt_ready, 1)
                dve.wait_ge(kt_ready, 1)
                own(nc.vector.tensor_tensor(kblk[:, 0], kt[:, 0:CTX].unsqueeze(1).broadcast_to([D, H, CTX]),
                                            cst[:, C_HEAD:C_GROUP].unsqueeze(2).broadcast_to([D, H, CTX]), ALU.mult))
                flat = kblk[:, 0].rearrange("p h k -> p (h k)")
                own(nc.vector.tensor_copy(kblk_hi[:, 0], flat))
                nc.vector.tensor_tensor(kblk_lo[:, 0], flat, kblk_hi[:, 0].bitcast(F32), ALU.subtract).then_inc(kblk0_ready, 1)

            def setup_values():
                dve.wait_ge(v_done, 1)
                dve.wait_ge(in_bias, 16 * 3)
                own(nc.vector.tensor_tensor(vrep[:, :, :], pv[:, :].rearrange("p (b d) -> p b d", b=B),
                                            bv_s[:, :].unsqueeze(1).broadcast_to([P, B, D]), ALU.add))
                groups = cst[:, C_GROUP:C_ONES].unsqueeze(1).unsqueeze(3).broadcast_to([P, B * NG, GH, HD])
                nc.vector.tensor_tensor(vblk[:, :, :].rearrange("p b (g j d) -> p (b g) j d", g=NG, j=GH),
                                        vrep[:, :, :].rearrange("p b (g j d) -> p (b g) j d", g=NG, j=GH),
                                        groups, ALU.mult).then_inc(vblk_ready, 1)

            def setup_experts():
                dve.wait_ge(upw_hi, 1)
                nc.vector.tensor_tensor(wup_lo[:, :], wup[:, :], wup_hi[:, :].bitcast(F32), ALU.subtract)
                dve.wait_ge(in_router, 16)
                own(nc.vector.tensor_copy(rt_hi[:, :], rt[:, :]))
                nc.vector.tensor_tensor(rt_lo[:, :], rt[:, :], rt_hi[:, :].bitcast(F32), ALU.subtract).then_inc(upw_lo, 1)

            def attention(b, s):
                if s == 0:
                    dve.wait_ge(in_x[b], 16)
                    layernorm_stats(xin[:, b], 0, stats_ready)
                if s == 1:
                    dve.wait_ge(rstd_ready, b + 1)
                    layernorm_apply(xn, xin[:, b], 0, xn_ready)
                if s == 2:
                    dve.wait_ge(qhi_ready, b + 1)
                    nc.vector.scalar_tensor_tensor(qt_lo[:, :], mx[:, :], bq_s[:, :], qt_hi[:, :].bitcast(F32),
                                                   ALU.add, ALU.subtract).then_inc(qlo_ready, 1)
                if 3 <= s < 3 + NT:
                    j = s - 3
                    if j == 0 and b == 0:
                        dve.wait_ge(in_mask, 16)
                    dve.wait_ge(s_done, NT * b + j + 1)
                    nc.vector.scalar_tensor_tensor(score[:, j], msk[:, b, j].unsqueeze(1).broadcast_to([P, H, CTX]), MASK_SCALE,
                                                   sc[:, :].rearrange("p (h k) -> p h k", h=H),
                                                   ALU.mult, ALU.add).then_inc(score_evac, 1)
                    dve.wait_ge(score_evac, NT * b + j + 1)
                    nc.vector.tensor_reduce(rowmax[:, j], score[:, j], AX_X, ALU.max).then_inc(max_ready, 1)
                if s == 13:
                    dve.wait_ge(pv_done, b + 1)
                    own(nc.vector.reciprocal(rsum[:, :], mx[:, :]))
                    nc.vector.tensor_tensor(ot[:, :], pv[:, :], rsum[:, :], ALU.mult).then_inc(ot_ready, 1)
                if s == 15:
                    dve.wait_ge(wo_done, b + 1)
                    dve.wait_ge(xb_ready, b + 1)
                    nc.vector.tensor_tensor(x2[:, b], tp[:, :].rearrange("p (j d) -> p j d", j=NT), xb[:, b],
                                            ALU.add).then_inc(x2_ready, 1)
                    dve.wait_ge(x2_ready, b + 1)
                    layernorm_stats(x2[:, b], 1, stats2_ready)
                if s == 16:
                    dve.wait_ge(rstd2_ready, b + 1)
                    layernorm_apply(xn2, x2[:, b], 1, xn2_ready)
                if s == 17:
                    dve.wait_ge(x2hi_ready, b + 1)
                    nc.vector.tensor_tensor(x2t_lo[:, :], tp[:, :], x2t_hi[:, :].bitcast(F32), ALU.subtract).then_inc(x2lo_ready, 1)

            def route(f):
                dve.wait_ge(logit_done, f + 1)
                nc.vector.tensor_tensor(logit[:, :, :], mx[:, 0:NT * E].rearrange("p (j e) -> p j e", j=NT),
                                        rb_s[:, :].unsqueeze(1).broadcast_to([P, NT, E]), ALU.add).then_inc(logit_ready, 1)
                dve.wait_ge(logit_ready, f + 1)
                for j in range(NT):
                    last = nc.vector.max(top[:, j, :], logit[:, j, :])
                own(last)
                nc.vector.tensor_tensor(lead[:, :], top[:, :, 0], top[:, :, 1], ALU.subtract).then_inc(lead_ready, 1)
                for j in range(NT):
                    last = nc.vector.max_index(topi[:, j, :], top[:, j, :], logit[:, j, :])
                own(last)
                for k in range(TOPK):
                    last = nc.vector.tensor_tensor(hot[:, k], cst[:, C_IOTA:C_PICK].unsqueeze(1).broadcast_to([P, NT, E]),
                                                   topi[:, :, k:k + 1].broadcast_to([P, NT, E]), ALU.is_equal)
                dve.wait_ge(tanh_ready, f + 1)
                nc.vector.tensor_scalar(topw[:, :, 0], tanh[:, :], 0.5, 0.5, ALU.mult, ALU.add)
                own(nc.vector.tensor_scalar(topw[:, :, 1], tanh[:, :], -0.5, 0.5, ALU.mult, ALU.add))
                for k in range(TOPK):
                    last = nc.vector.tensor_tensor(hot[:, k], hot[:, k], topw[:, :, k:k + 1].broadcast_to([P, NT, E]), ALU.mult)
                own(last)
                own(nc.vector.tensor_tensor(comb[:, :, :], hot[:, 0], hot[:, 1], ALU.add))
                own(nc.vector.tensor_copy(parts[:, :, 0, :], comb[:, :, :]))
                own(nc.vector.tensor_tensor(rest1[:, :, :], comb[:, :, :], parts[:, :, 0, :], ALU.subtract))
                own(nc.vector.tensor_copy(parts[:, :, 1, :], rest1[:, :, :]))
                own(nc.vector.tensor_tensor(rest2[:, :, :], rest1[:, :, :], parts[:, :, 1, :], ALU.subtract))
                nc.vector.tensor_copy(parts[:, :, 2, :], rest2[:, :, :]).then_inc(parts_ready, 1)
                dve.wait_ge(ct_done, f + 1)
                nc.vector.tensor_copy(combt[:, :], tp[0:PARTS * E, 0:S // 2].bitcast(BF16)).then_inc(combt_ready, 1)

            def scale_chunk(n):
                e = n % NU // FC
                dve.wait_ge(silu_ready, n + 1)
                dve.wait_ge(cbc_done, (n // NU) * E + e)
                if n >= 4:
                    dve.wait_ge(down_done, n - 3)
                nc.vector.tensor_tensor(act_in[:, n % 4], silu[:, n % 4], cbc[:, :], ALU.mult).then_inc(scaled_ready, 1)

            for w in range(B + 1):
                f = w - 1
                if f >= 0:
                    route(f)
                for s in range(NU):
                    if f >= 0 and s % 2 == 0 and s >= FC:
                        for c in range(FC):
                            scale_chunk(NU * f + s + c)
                    if w < B:
                        attention(w, s)
                    if w == 0 and s == 0:
                        setup_keys()
                    if w == 0 and s == 2:
                        setup_values()
                    if w == 0 and s == 7:
                        setup_experts()
                    if f >= 1 and s == 1:
                        dve.wait_ge(outt_done, f)
                        nc.vector.tensor_tensor(res[:, f - 1], pv[:, :].rearrange("p (j d) -> p j d", j=NT), x2[:, f - 1],
                                                ALU.add).then_inc(res_ready, 1)
            dve.wait_ge(outt_done, B)
            nc.vector.tensor_tensor(res[:, B - 1], pv[:, :].rearrange("p (j d) -> p j d", j=NT), x2[:, B - 1],
                                    ALU.add).then_inc(res_ready, 1)

        @block.tensor
        def _(pe):
            def split_product(dst, stationary, moving):
                (s_hi, s_lo), (m_hi, m_lo) = stationary, moving
                nc.tensor.matmul(dst, s_hi, m_hi, start=True, stop=False)
                nc.tensor.matmul(dst, s_lo, m_hi, start=False, stop=False)
                return nc.tensor.matmul(dst, s_hi, m_lo, start=False, stop=True)

            def up(n):
                c = n % NU
                if n >= FC:
                    pe.wait_ge(silu_ready, n - FC + 1)
                w = slice(c * P, (c + 1) * P)
                split_product(hid[n % FC][:, :], (wup_hi[:, w], wup_lo[:, w]), (x2t_hi[:, :], x2t_lo[:, :])).then_inc(up_done, 1)

            def down(n):
                c = n % NU
                if c == 0 and n:
                    pe.wait_ge(yt_ready, n // NU)
                if c < FC:
                    pe.wait_ge(silu_ready, n + 1)
                else:
                    pe.wait_ge(scaled_ready, scaled_upto(n))
                nc.tensor.matmul(yacc[:, :], wdn[:, c, :], act_in[:, n % 4], start=(c == 0), stop=(c == NU - 1)).then_inc(down_done, 1)

            def broadcast_weights(f, e):
                if e == 1:
                    pe.wait_ge(combt_ready, f + 1)
                n = NU * f + FC * e - 1
                if scaled_upto(n) > 0:
                    pe.wait_ge(scaled_ready, scaled_upto(n))
                nc.tensor.matmul(cbc[:, :], pick[:, (e - 1) * P:e * P], combt[:, :], start=True, stop=True).then_inc(cbc_done, 1)

            def turn_output(f):
                pe.wait_ge(yt_ready, f + 1)
                for j in range(NT):
                    last = nc.tensor.transpose(pv[:, j * P:(j + 1) * P], yt[:, j * P:(j + 1) * P], ident)
                last.then_inc(outt_done, 1)

            def route(f):
                pe.wait_ge(x2lo_ready, f + 1)
                for j in range(NT):
                    t = slice(j * P, (j + 1) * P)
                    last = split_product(mx[:, j * E:(j + 1) * E], (x2t_hi[:, t], x2t_lo[:, t]), (rt_hi[:, :], rt_lo[:, :]))
                last.then_inc(logit_done, 1)

            def turn_weights(f):
                pe.wait_ge(parts_ready, f + 1)
                for j in range(NT):
                    last = nc.tensor.transpose(tp[0:PARTS * E, j * P // 2:(j + 1) * P // 2].bitcast(BF16),
                                               parts[:, j].rearrange("p a e -> p (a e)"), ident16[:, :])
                last.then_inc(ct_done, 1)

            def attention(b, s):
                if s == 1:
                    pe.wait_ge(xn_ready, b + 1)
                    for j in range(NT):
                        last = nc.tensor.transpose(tp[:, j * P:(j + 1) * P], xn[:, j, :], ident)
                    last.then_inc(xt_done, 1)
                if s == 2:
                    if b == 0:
                        pe.wait_ge(in_wq, 32)
                        pe.wait_ge(kt_ready, 1)
                    else:
                        pe.wait_ge(logit_ready, b)
                    pe.wait_ge(xnt_copied, b + 1)
                    nc.tensor.matmul(mx[:, :], wq_s[:, :], xnt[:, :], start=True, stop=True).then_inc(q_done, 1)
                if 3 <= s < 3 + NT:
                    j = s - 3
                    if j == 0:
                        pe.wait_ge(qlo_ready, b + 1)
                        if b == 0:
                            pe.wait_ge(kblk0_ready, 1)
                        else:
                            pe.wait_ge(kblk_ready, b)
                    if NT * b + j:
                        pe.wait_ge(score_evac, NT * b + j)
                    t = slice(j * P, (j + 1) * P)
                    split_product(sc[:, :], (qt_hi[:, t], qt_lo[:, t]), (kblk_hi[:, b], kblk_lo[:, b])).then_inc(s_done, 1)
                if 9 <= s < 9 + NT:
                    j = s - 9
                    pe.wait_ge(prob_ready, b + 1)
                    if j:
                        pe.wait_ge(pt_copied, NT * b + j)
                    for g in range(NG):
                        last = nc.tensor.transpose(tp[:, g * P:(g + 1) * P], prob[:, j, g * P:(g + 1) * P], ident)
                    last.then_inc(ptr_done, 1)
                if s == 13:
                    pe.wait_ge(pt_copied, NT * (b + 1))
                    if b == 0:
                        pe.wait_ge(vblk_ready, 1)
                    if b >= 2:
                        pe.wait_ge(res_ready, b - 1)
                    for g in range(NG):
                        rows = slice(g * CTX, (g + 1) * CTX)
                        nc.tensor.matmul(pv[rows, :], vblk[:, b, rows], probt[:, g, :], start=True, stop=True)
                    for g in range(NG):
                        rows = slice(g * CTX, (g + 1) * CTX)
                        last = nc.tensor.matmul(mx[rows, :], cst[:, C_ONES:C_IOTA], probt[:, g, :], start=True, stop=True)
                    last.then_inc(pv_done, 1)
                if s == 15:
                    pe.wait_ge(ot_ready, b + 1)
                    if b == 0:
                        pe.wait_ge(in_wo, 16)
                    for j in range(NT):
                        last = nc.tensor.matmul(tp[:, j * D:(j + 1) * D], ot[:, j * P:(j + 1) * P], wo_s[:, :], start=True, stop=True)
                    last.then_inc(wo_done, 1)
                if s == 17:
                    pe.wait_ge(xn2_ready, b + 1)
                    for j in range(NT):
                        last = nc.tensor.transpose(tp[:, j * P:(j + 1) * P], xn2[:, j, :], ident)
                    last.then_inc(x2t_done, 1)

            pe.wait_ge(in_ctx, 32)
            pe.wait_ge(in_kv, 48)
            nc.tensor.matmul(mx[:, 0:B * CTX], wk_s[:, :], ctxt[:, :], start=True, stop=True).then_inc(k_done, 1)
            for b in range(B):
                last = nc.tensor.matmul(pv[:, b * D:(b + 1) * D], ctxrep[:, b].rearrange("d j k -> d (j k)"), wv_s[:, :],
                                        start=True, stop=True)
            last.then_inc(v_done, 1)
            pe.wait_ge(in_cst, 16)
            pe.wait_ge(const_ready, 1)
            for w in range(B + 1):
                f = w - 1
                if f >= 0:
                    route(f)
                    if f == 0:
                        pe.wait_ge(upw_lo, 1)
                    for c in range(FC):
                        up(NU * f + c)
                    if f >= 1:
                        turn_output(f - 1)
                for s in range(NU):
                    e = s // 2
                    if f >= 0 and s % 2 == 0 and e + 1 < NE:
                        for c in range(FC):
                            up(NU * f + FC * (e + 1) + c)
                        if e == 0:
                            turn_weights(f)
                            broadcast_weights(f, 1)
                            if f == 0:
                                pe.wait_ge(in_down, 16)
                    if f >= 0 and s % 2 == 1:
                        down(NU * f + FC * e)
                        if e >= 1 and e + 1 < NE:
                            broadcast_weights(f, e + 1)
                        down(NU * f + FC * e + 1)
                    if w < B:
                        attention(w, s)
            turn_output(B - 1)


def kernel(**inputs):
    import numpy as _np
    import concourse.bacc as _bacc
    from concourse import mybir as _mybir
    from concourse.bass_utils import run_bass_kernel_spmd as _run

    a = {k: _np.asarray(v) for k, v in inputs.items()}
    w_up = _np.concatenate([a["L0_ffn_shared_w_up"], a["L0_ffn_w_up"]])
    w_down = _np.concatenate([a["L0_ffn_shared_w_down"], a["L0_ffn_w_down"]])
    ctx_t = _np.broadcast_to(a["ctx_1024"].transpose(2, 0, 1)[:, :, None, :], (D, B, GH, CTX))
    laid_out = {
        "x": a["x"],
        "ctx_t": ctx_t,
        "mask": a["mask_Bx1xSxS2_ff0"],
        "wq": a["L0_xattn_Wq"], "bq": a["L0_xattn_bq"],
        "wk": a["L0_xattn_Wk"], "bk": a["L0_xattn_bk"],
        "wv": a["L0_xattn_Wv"], "bv": a["L0_xattn_bv"],
        "wo": a["L0_xattn_Wo"], "bo": a["L0_xattn_bo"],
        "router_t": a["L0_ffn_router_w"].T, "router_b": a["L0_ffn_router_b"],
        "w_up_t": w_up.reshape(NE * F, D).T,
        "w_down_t": w_down.reshape(NE, D, FC, P).transpose(3, 0, 2, 1).reshape(P, NU, D),
        "consts": shape_constants(),
    }
    nc = _bacc.Bacc("TRN2", target_bir_lowering=False, num_devices=1)
    arrays, args = {}, []
    for name, value in laid_out.items():
        value = _np.ascontiguousarray(value)
        arrays[f"in_{name}"] = value
        args.append(nc.dram_tensor(f"in_{name}", value.shape, _mybir.dt.from_np(value.dtype), kind="ExternalInput").ap())
    args.append(nc.dram_tensor("out_0", (B, S, D), _mybir.dt.float32, kind="ExternalOutput").ap())
    xattn_moe(nc, *args)
    r = _run(nc, [arrays], core_ids=[0])
    return r.results[0]["out_0"]
```

```python
from contextlib import ExitStack

import numpy as np

import concourse.bass as bass
from concourse import mybir

F32 = mybir.dt.float32
F32R = mybir.dt.float32r
BF16 = mybir.dt.bfloat16
U32 = mybir.dt.uint32
ALU = mybir.AluOpType
ACT = mybir.ActivationFunctionType
AX_X = mybir.AxisListType.X

P = 128
B, S, D = 4, 512, 128
CTX = 32
H, HD = 16, 8
GH = P // CTX
NG = H // GH
NT = S // P
E, F = 8, 256
NE = E + 1
FC = F // P
NU = NE * FC
TOPK = 2
WCUT = 3
RING, LONG = 4, 6
PARTS = 3
SCALE = 1.0 / float(np.sqrt(np.float32(D)))
MASK_SCALE = -1000000000.0
LN_EPS = 1e-5

C_IDENT = 0
C_HEAD = C_IDENT + P
C_GROUP = C_HEAD + H
C_IOTA = C_GROUP + GH
C_END = C_IOTA + E

UP0 = 12
DOWN_LAG = 5
SLOTS_OF_BATCH = 2 * NE
NK = B * NE
OUT_LAG = 2 * NE + DOWN_LAG - 1
SLOTS = UP0 + SLOTS_OF_BATCH * (B - 1) + OUT_LAG + 3
FIRST = dict(stats=0, apply=0, xt=1, xcopy=1, q=2, qhi=2, qlo=2,
             score=[3, 4, 5, 6], evac=[3, 4, 5, 6], shift=[3, 4, 5, 6], exp=[3, 4, 5, 6],
             rowsum=[4, 5, 6, 7], norm=[4, 5, 6, 7], pt=[5, 6, 7, 8],
             pv=9, ot=9, wo=10, x2=10, apply2=10, x2t=11, x2hi=11, x2lo=11,
             logit=12, top=12, tanh=12, weigh=12, turn=13, turned=13)
SECOND = dict(stats=0, apply=1, xt=2, xcopy=2, q=3, qhi=3, qlo=4,
              score=[5, 6, 7, 8], evac=[6, 7, 8, 9], shift=[6, 7, 8, 9], exp=[11, 11, 11, 11],
              rowsum=[12, 12, 12, 12], norm=[12, 12, 13, 13], pt=[14, 15, 16, 17],
              pv=18, ot=18, wo=19, x2=20, apply2=21, x2t=22, x2hi=22, x2lo=22,
              logit=23, top=24, tanh=24, weigh=25, turn=26, turned=26)
LATER = dict(stats=0, apply=1, xt=2, xcopy=2, q=3, qhi=3, qlo=4,
             score=[5, 6, 7, 8], evac=[6, 7, 8, 9], shift=[6, 7, 8, 9], exp=[10, 10, 10, 10],
             rowsum=[13, 13, 14, 14], norm=[14, 14, 15, 15], pt=[15, 16, 17, 18],
             pv=19, ot=19, wo=21, x2=22, apply2=23, x2t=24, x2hi=24, x2lo=25,
             logit=26, top=27, tanh=27, weigh=27, turn=28, turned=29)
BEGINS = [0, 5] + [UP0 + SLOTS_OF_BATCH * b - 28 for b in range(2, B)]


def due(b, slot, stage, j=None):
    at = (FIRST, SECOND, LATER)[min(b, 2)][stage]
    return slot - BEGINS[b] == (at if j is None else at[j])


def shape_constants():
    c = np.zeros((P, C_END), np.float32)
    p = np.arange(P)
    c[:, C_IDENT:C_HEAD] = np.eye(P, dtype=np.float32)
    c[:, C_HEAD:C_GROUP] = p[:, None] // HD == np.arange(H)[None, :]
    c[:, C_GROUP:C_IOTA] = p[:, None] // CTX == np.arange(GH)[None, :]
    c[:, C_IOTA:C_END] = np.arange(E)[None, :]
    return c


def expert_constants():
    rows = np.arange(PARTS * E)
    pick = rows[:, None] % E == np.arange(E)[None, :]
    return np.repeat(pick, P, axis=1).astype(np.float32)


def xattn_moe(nc: bass.Bass, x, ctx_t, mask, wq, bq, wk, bk, wv, bv, wo, bo,
              router_t, router_b, w_up_t, w_down_t, consts, pick_const, out):
    with ExitStack() as stack:
        def sb(name, shape, dt=F32):
            return stack.enter_context(nc.sbuf_tensor(name, shape, dt))

        def bank(name):
            return stack.enter_context(nc.psum_tensor(name, [P, S], F32))

        def sem(name):
            return stack.enter_context(nc.semaphore(name))

        cst = sb("cst", [P, C_END])
        ident = cst[:, C_IDENT:C_HEAD]
        pick32 = sb("pick32", [PARTS * E, E * P])
        pick = sb("pick", [PARTS * E, E * P], BF16)
        ident16 = sb("ident16", [P, P], BF16)
        xin = sb("xin", [P, B, NT, D])
        msk = sb("msk", [P, B, NT, CTX])
        ctxt = sb("ctxt", [D, B, CTX])
        ctxrep = sb("ctxrep", [D, B, GH, CTX])
        wq_s, wk_s, wv_s, wo_s = sb("wq_s", [D, D]), sb("wk_s", [D, D]), sb("wv_s", [D, D]), sb("wo_s", [D, D])
        bq_s, bk_s = sb("bq_s", [D, 1]), sb("bk_s", [D, 1])
        bv_s, bo_s, rb_s = sb("bv_s", [P, D]), sb("bo_s", [P, D]), sb("rb_s", [P, E])
        rt = sb("rt", [D, E])
        rt_hi, rt_lo = sb("rt_hi", [D, E], F32R), sb("rt_lo", [D, E], F32R)
        wup, wup_hi, wup_lo = (sb(n, [D, WCUT, NU * P // WCUT], t) for n, t in (("wup", F32), ("wup_hi", F32R), ("wup_lo", F32R)))
        wdn, wdn_hi, wdn_lo = (sb(n, [P, WCUT, NU * D // WCUT], t) for n, t in (("wdn", F32), ("wdn_hi", F32R), ("wdn_lo", F32R)))
        kt = sb("kt", [D, B, CTX])
        kblk = sb("kblk", [D, 2, H, CTX])
        kblk_hi, kblk_lo = sb("kblk_hi", [D, B, H * CTX], F32R), sb("kblk_lo", [D, B, H * CTX], F32R)
        vrep = sb("vrep", [P, B, D])
        vblk = sb("vblk", [P, B, D])
        minus_half = sb("minus_half", [P, NT])
        stats = sb("stats", [P, NT, 6])
        mv = sb("mv", [P, 2, NT, 2])
        vareps = sb("vareps", [P, NT])
        rstd = sb("rstd", [P, 2, NT])
        xn = sb("xn", [P, NT, D])
        xnt = sb("xnt", [D, S])
        qt_hi, qt_lo = sb("qt_hi", [D, S], F32R), sb("qt_lo", [D, S], F32R)
        score = sb("score", [P, NT, H, CTX])
        rowmax = sb("rowmax", [P, NT, H])
        prob = sb("prob", [P, NT, H, CTX])
        rowsum, rsum = sb("rowsum", [P, NT, H]), sb("rsum", [P, NT, H])
        probt = sb("probt", [P, NG, S])
        ot = sb("ot", [D, S])
        xb = sb("xb", [P, B, NT, D])
        x2 = sb("x2", [P, B, NT, D])
        xn2 = sb("xn2", [P, NT, D])
        x2t_hi, x2t_lo = sb("x2t_hi", [D, 2, S], F32R), sb("x2t_lo", [D, 2, S], F32R)
        logit = sb("logit", [P, NT, E])
        top = sb("top", [P, NT, 8])
        topi = sb("topi", [P, NT, 8], U32)
        lead = sb("lead", [P, NT])
        tanh = sb("tanh", [P, NT])
        topw = sb("topw", [P, NT, TOPK])
        hot = sb("hot", [P, TOPK, NT, E])
        comb = sb("comb", [P, NT, E])
        rest1, rest2 = sb("rest1", [P, NT, E]), sb("rest2", [P, NT, E])
        parts = sb("parts", [P, NT, PARTS, E], BF16)
        combt = sb("combt", [PARTS * E, S], BF16)
        silu = sb("silu", [P, RING, S])
        hin = sb("hin", [P, RING, S])
        hin_hi, hin_lo = sb("hin_hi", [P, LONG, S], F32R), sb("hin_lo", [P, LONG, S], F32R)
        yt = sb("yt", [D, S])

        hid = [bank("hid0"), bank("hid1")]
        yacc = bank("yacc")
        cbc = bank("cbc")
        turn_a, turn_b = bank("turn_a"), bank("turn_b")
        sc_a, sc_b = bank("sc_a"), bank("sc_b")

        in_x = [sem(f"in_x{b}") for b in range(B)]
        in_ctx, in_cst, in_wq, in_wk, in_wv, in_mask = sem("in_ctx"), sem("in_cst"), sem("in_wq"), sem("in_wk"), sem("in_wv"), sem("in_mask")
        in_bv, in_bo, in_wo, in_router, in_up, in_down = sem("in_bv"), sem("in_bo"), sem("in_wo"), sem("in_router"), sem("in_up"), sem("in_down")
        out_stored = sem("out_stored")
        k_done, v_done = sem("k_done"), sem("v_done")
        xt_done, q_done, s_done, ptr_done, pv_done = sem("xt_done"), sem("q_done"), sem("s_done"), sem("ptr_done"), sem("pv_done")
        wo_done, x2t_done, logit_done, ct_done, cbc_done = sem("wo_done"), sem("x2t_done"), sem("logit_done"), sem("ct_done"), sem("cbc_done")
        up_done, down_done, outt_done = sem("up_done"), sem("down_done"), sem("outt_done")
        ctxrep_ready, upw_hi, downw_hi = sem("ctxrep_ready"), sem("upw_hi"), sem("downw_hi")
        xnt_copied, qhi_ready, prob_ready, pt_copied, ot_ready = sem("xnt_copied"), sem("qhi_ready"), sem("prob_ready"), sem("pt_copied"), sem("ot_ready")
        x2hi_ready, tanh_ready, silu_ready, hi_ready, yt_ready = sem("x2hi_ready"), sem("tanh_ready"), sem("silu_ready"), sem("hi_ready"), sem("yt_ready")
        dve_step = sem("dve_step")
        kt_ready, kblk0_ready, vblk_ready, const_ready, upw_lo = sem("kt_ready"), sem("kblk0_ready"), sem("vblk_ready"), sem("const_ready"), sem("upw_lo")
        stats_ready, xn_ready, qlo_ready, max_ready, rsum_ready = sem("stats_ready"), sem("xn_ready"), sem("qlo_ready"), sem("max_ready"), sem("rsum_ready")
        score_evac = sem("score_evac")
        x2_ready, stats2_ready, xn2_ready, x2lo_ready = sem("x2_ready"), sem("stats2_ready"), sem("xn2_ready"), sem("x2lo_ready")
        logit_ready, lead_ready, parts_ready, combt_ready, scaled_ready = sem("logit_ready"), sem("lead_ready"), sem("parts_ready"), sem("combt_ready"), sem("scaled_ready")
        lo0_ready, res_ready = sem("lo0_ready"), sem("res_ready")
        pool_step = sem("pool_step")
        rstd_ready, rstd2_ready, shifted_ready, normed_ready = sem("rstd_ready"), sem("rstd2_ready"), sem("shifted_ready"), sem("normed_ready")
        xb_ready, kblk_ready, downw_lo, lo1_ready = sem("xb_ready"), sem("kblk_ready"), sem("downw_lo"), sem("lo1_ready")

        def shared(k):
            return k % NE == 0

        def scaled_upto(n):
            return (n // NU) * (NU - FC) + max(0, n % NU - FC + 1)

        def expert_in(slot):
            k = (slot - UP0) // 2
            return k

        block = stack.enter_context(nc.Block())

        @block.sync
        def _(sp):
            sp.dma_start(xin[:, 0], x[0].rearrange("(p j) d -> p j d", j=NT)).then_inc(in_x[0], 16)
            sp.dma_start(cst[:, :], consts).then_inc(in_cst, 16)
            sp.dma_start(wq_s[:, :], wq).then_inc(in_wq, 16)
            sp.dma_start(bq_s[:, :], bq.rearrange("(d a) -> d a", a=1)).then_inc(in_wq, 16)
            sp.dma_start(msk[:, :, :, :], mask.rearrange("b a (p j) k -> p (b a) j k", j=NT)).then_inc(in_mask, 16)
            sp.dma_start(wup[:, :, :], w_up_t).then_inc(in_up, 16)
            sp.dma_start(xin[:, 1], x[1].rearrange("(p j) d -> p j d", j=NT)).then_inc(in_x[1], 16)
            sp.dma_start(wdn[:, :, :], w_down_t).then_inc(in_down, 16)
            for b in range(2, B):
                sp.dma_start(xin[:, b], x[b].rearrange("(p j) d -> p j d", j=NT)).then_inc(in_x[b], 16)
            for b in range(B):
                sp.wait_ge(res_ready, b + 1)
                sp.dma_start(out[b].rearrange("(p j) d -> p j d", j=NT), x2[:, b]).then_inc(out_stored, 16)
            sp.wait_ge(out_stored, 16 * B)

        @block.gpsimd
        def _(pool):
            steps = [0]

            def own(ins):
                steps[0] += 1
                ins.then_inc(pool_step, 1)
                pool.wait_ge(pool_step, steps[0])

            def root(which, done):
                own(nc.gpsimd.tensor_scalar(vareps[:, :], mv[:, which, :, 1], LN_EPS, None, ALU.add))
                nc.gpsimd.tensor_tensor(rstd[:, which, :], vareps[:, :], minus_half[:, :], ALU.pow).then_inc(done, 1)

            def attention(b, slot):
                if due(b, slot, "stats"):
                    pool.wait_ge(stats_ready, b + 1)
                    root(0, rstd_ready)
                for j in range(NT):
                    if due(b, slot, "shift", j):
                        pool.wait_ge(max_ready, NT * b + j + 1)
                        nc.gpsimd.tensor_tensor(score[:, j], score[:, j], rowmax[:, j].unsqueeze(2).broadcast_to([P, H, CTX]),
                                                ALU.subtract).then_inc(shifted_ready, 1)
                for j in range(NT):
                    if due(b, slot, "norm", j):
                        pool.wait_ge(rsum_ready, NT * b + j + 1)
                        nc.gpsimd.tensor_tensor(prob[:, j], prob[:, j], rsum[:, j].unsqueeze(2).broadcast_to([P, H, CTX]),
                                                ALU.mult).then_inc(normed_ready, 1)
                if due(b, slot, "ot"):
                    if b == 0:
                        pool.wait_ge(in_bo, 16)
                    pool.wait_ge(in_x[b], 16)
                    nc.gpsimd.tensor_tensor(xb[:, b], xin[:, b], bo_s[:, :].unsqueeze(1).broadcast_to([P, NT, D]),
                                            ALU.add).then_inc(xb_ready, 1)
                if due(b, slot, "x2"):
                    pool.wait_ge(stats2_ready, b + 1)
                    root(1, rstd2_ready)

            def block_keys(b):
                if b > 1:
                    pool.wait_ge(kblk_ready, b - 1)
                pool.wait_ge(kt_ready, 1)
                own(nc.gpsimd.tensor_tensor(kblk[:, 1], kt[:, b].unsqueeze(1).broadcast_to([D, H, CTX]),
                                            cst[:, C_HEAD:C_GROUP].unsqueeze(2).broadcast_to([D, H, CTX]), ALU.mult))
                flat = kblk[:, 1].rearrange("p h k -> p (h k)")
                own(nc.gpsimd.tensor_copy(kblk_hi[:, b], flat))
                nc.gpsimd.tensor_tensor(kblk_lo[:, b], flat, kblk_hi[:, b].bitcast(F32), ALU.subtract).then_inc(kblk_ready, 1)

            own(nc.gpsimd.memset(minus_half[:, :], -0.5))
            for slot in range(SLOTS):
                k = expert_in(slot) - 1
                if slot % 2 == 0 and 0 <= k < NK:
                    n = FC * k + 1
                    pool.wait_ge(hi_ready, n + 1)
                    nc.gpsimd.tensor_tensor(hin_lo[:, n % LONG], hin[:, n % RING], hin_hi[:, n % LONG].bitcast(F32),
                                            ALU.subtract).then_inc(lo1_ready, 1)
                for b in range(B):
                    attention(b, slot)
                if slot == 0:
                    for b in range(1, B):
                        block_keys(b)
                if 10 <= slot < 10 + WCUT:
                    c = slot - 10
                    pool.wait_ge(downw_hi, c + 1)
                    nc.gpsimd.tensor_tensor(wdn_lo[:, c], wdn[:, c], wdn_hi[:, c].bitcast(F32), ALU.subtract).then_inc(downw_lo, 1)

        @block.scalar
        def _(act):
            act.dma_start(ctxt[:, :, :], ctx_t).then_inc(in_ctx, 16)
            act.dma_start(wk_s[:, :], wk).then_inc(in_wk, 16)
            act.dma_start(bk_s[:, :], bk.rearrange("(d a) -> d a", a=1)).then_inc(in_wk, 16)
            act.dma_start(wv_s[:, :], wv).then_inc(in_wv, 16)
            act.dma_start(bv_s[:, :], bv.partition_broadcast(P)).then_inc(in_bv, 16)
            act.dma_start(wo_s[:, :], wo).then_inc(in_wo, 16)
            act.dma_start(bo_s[:, :], bo.partition_broadcast(P)).then_inc(in_bo, 16)
            act.dma_start(rb_s[:, :], router_b.partition_broadcast(P)).then_inc(in_router, 16)
            act.dma_start(rt[:, :], router_t).then_inc(in_router, 16)
            act.dma_start(pick32[:, :], pick_const).then_inc(in_router, 16)

            def silu_chunk(n):
                act.wait_ge(up_done, n + 1)
                if shared(n // FC):
                    if n >= RING:
                        act.wait_ge((lo0_ready, lo1_ready)[n % FC], (n - RING) // FC + 1)
                    nc.scalar.activation(hin[:, n % RING], hid[n % FC][:, :], ACT.Silu).then_inc(silu_ready, 1)
                else:
                    if n >= RING and scaled_upto(n - RING) > 0:
                        act.wait_ge(scaled_ready, scaled_upto(n - RING))
                    nc.scalar.activation(silu[:, n % RING], hid[n % FC][:, :], ACT.Silu).then_inc(silu_ready, 1)

            def round_chunk(n):
                if shared(n // FC):
                    act.wait_ge(silu_ready, n + 1)
                else:
                    act.wait_ge(scaled_ready, scaled_upto(n))
                if n >= LONG:
                    act.wait_ge(down_done, n - LONG + 1)
                nc.scalar.activation(hin_hi[:, n % LONG], hin[:, n % RING], ACT.Copy).then_inc(hi_ready, 1)

            def attention(b, slot):
                if due(b, slot, "xcopy"):
                    act.wait_ge(xt_done, b + 1)
                    nc.scalar.activation(xnt[:, :], turn_a[:, :], ACT.Copy).then_inc(xnt_copied, 1)
                if due(b, slot, "qhi"):
                    act.wait_ge(q_done, b + 1)
                    nc.scalar.activation(qt_hi[:, :], turn_b[:, :], ACT.Identity, bias=bq_s[:, :]).then_inc(qhi_ready, 1)
                for j in range(NT):
                    if due(b, slot, "exp", j):
                        act.wait_ge(shifted_ready, NT * b + j + 1)
                        nc.scalar.activation(prob[:, j], score[:, j], ACT.Exp).then_inc(prob_ready, 1)
                for j in range(NT):
                    if due(b, slot, "pt", j):
                        act.wait_ge(ptr_done, NT * b + j + 1)
                        nc.scalar.activation(probt[:, :, j * P:(j + 1) * P],
                                             (turn_a, turn_b)[j % 2][:, :].rearrange("p (g t) -> p g t", g=NG),
                                             ACT.Copy).then_inc(pt_copied, 1)
                if due(b, slot, "ot"):
                    act.wait_ge(pv_done, b + 1)
                    nc.scalar.activation(ot[:, :], sc_a[:, :], ACT.Copy).then_inc(ot_ready, 1)
                if due(b, slot, "x2hi"):
                    act.wait_ge(x2t_done, b + 1)
                    nc.scalar.activation(x2t_hi[:, b % 2], turn_a[:, :], ACT.Copy).then_inc(x2hi_ready, 1)
                if due(b, slot, "tanh"):
                    act.wait_ge(lead_ready, b + 1)
                    nc.scalar.activation(tanh[:, :], lead[:, :], ACT.Tanh, scale=0.5).then_inc(tanh_ready, 1)

            act.wait_ge(in_ctx, 16)
            nc.scalar.activation(ctxrep[:, :, :, :], ctxt[:, :, :].unsqueeze(2).broadcast_to([D, B, GH, CTX]),
                                 ACT.Copy).then_inc(ctxrep_ready, 1)
            for slot in range(SLOTS):
                k = expert_in(slot)
                if 0 <= k < NK:
                    for c in range(FC):
                        (silu_chunk, round_chunk)[slot % 2](FC * k + c)
                f, s = divmod(slot - UP0 - OUT_LAG, SLOTS_OF_BATCH)
                if f >= 0 and s == 0 and f < B:
                    act.wait_ge(down_done, NU * (f + 1))
                    nc.scalar.activation(yt[:, :], yacc[:, :], ACT.Copy).then_inc(yt_ready, 1)
                for b in range(B):
                    attention(b, slot)
                if 3 <= slot < 3 + WCUT:
                    if slot == 3:
                        act.wait_ge(in_up, 16)
                    nc.scalar.activation(wup_hi[:, slot - 3], wup[:, slot - 3], ACT.Copy).then_inc(upw_hi, 1)
                if 7 <= slot < 7 + WCUT:
                    if slot == 7:
                        act.wait_ge(in_down, 16)
                    nc.scalar.activation(wdn_hi[:, slot - 7], wdn[:, slot - 7], ACT.Copy).then_inc(downw_hi, 1)

        @block.vector
        def _(dve):
            steps = [0]

            def own(ins):
                steps[0] += 1
                ins.then_inc(dve_step, 1)
                dve.wait_ge(dve_step, steps[0])

            def layernorm_stats(src, which, done):
                for j in range(NT):
                    last = nc.vector.bn_stats(stats[:, j, :], src[:, j, :])
                own(last)
                for j in range(NT):
                    last = nc.vector.bn_aggr(mv[:, which, j, :], stats[:, j, :])
                last.then_inc(done, 1)

            def layernorm_apply(dst, src, which, done):
                for j in range(NT):
                    last = nc.vector.tensor_scalar(dst[:, j, :], src[:, j, :], mv[:, which, j, 0:1], rstd[:, which, j:j + 1],
                                                   ALU.subtract, ALU.mult)
                last.then_inc(done, 1)

            def setup_keys():
                dve.wait_ge(in_cst, 16)
                dve.wait_ge(k_done, 1)
                nc.vector.tensor_scalar(kt[:, :, :].rearrange("p b k -> p (b k)"), hid[0][:, 0:B * CTX], bk_s[:, :], SCALE,
                                        ALU.add, ALU.mult).then_inc(kt_ready, 1)
                dve.wait_ge(kt_ready, 1)
                own(nc.vector.tensor_tensor(kblk[:, 0], kt[:, 0].unsqueeze(1).broadcast_to([D, H, CTX]),
                                            cst[:, C_HEAD:C_GROUP].unsqueeze(2).broadcast_to([D, H, CTX]), ALU.mult))
                flat = kblk[:, 0].rearrange("p h k -> p (h k)")
                own(nc.vector.tensor_copy(kblk_hi[:, 0], flat))
                nc.vector.tensor_tensor(kblk_lo[:, 0], flat, kblk_hi[:, 0].bitcast(F32), ALU.subtract).then_inc(kblk0_ready, 1)

            def setup_values():
                dve.wait_ge(v_done, 1)
                dve.wait_ge(in_bv, 16)
                own(nc.vector.tensor_tensor(vrep[:, :, :], yacc[:, :].rearrange("p (b d) -> p b d", b=B),
                                            bv_s[:, :].unsqueeze(1).broadcast_to([P, B, D]), ALU.add))
                groups = cst[:, C_GROUP:C_IOTA].unsqueeze(1).unsqueeze(3).broadcast_to([P, B * NG, GH, HD])
                nc.vector.tensor_tensor(vblk[:, :, :].rearrange("p b (g j d) -> p (b g) j d", g=NG, j=GH),
                                        vrep[:, :, :].rearrange("p b (g j d) -> p (b g) j d", g=NG, j=GH),
                                        groups, ALU.mult).then_inc(vblk_ready, 1)

            def setup_router():
                dve.wait_ge(in_router, 48)
                nc.vector.tensor_copy(pick[:, :], pick32[:, :])
                nc.vector.tensor_copy(ident16[:, :], ident)
                own(nc.vector.tensor_copy(rt_hi[:, :], rt[:, :]))
                nc.vector.tensor_tensor(rt_lo[:, :], rt[:, :], rt_hi[:, :].bitcast(F32), ALU.subtract).then_inc(const_ready, 1)

            def attention(b, slot):
                if due(b, slot, "stats"):
                    dve.wait_ge(in_x[b], 16)
                    layernorm_stats(xin[:, b], 0, stats_ready)
                    if b == 0:
                        setup_keys()
                if due(b, slot, "apply"):
                    dve.wait_ge(rstd_ready, b + 1)
                    layernorm_apply(xn, xin[:, b], 0, xn_ready)
                if due(b, slot, "qlo"):
                    dve.wait_ge(qhi_ready, b + 1)
                    nc.vector.scalar_tensor_tensor(qt_lo[:, :], turn_b[:, :], bq_s[:, :], qt_hi[:, :].bitcast(F32),
                                                   ALU.add, ALU.subtract).then_inc(qlo_ready, 1)
                for j in range(NT):
                    if due(b, slot, "evac", j):
                        if j == 0 and b == 0:
                            dve.wait_ge(in_mask, 16)
                        dve.wait_ge(s_done, NT * b + j + 1)
                        nc.vector.scalar_tensor_tensor(score[:, j], msk[:, b, j].unsqueeze(1).broadcast_to([P, H, CTX]), MASK_SCALE,
                                                       (sc_a, sc_b)[j % 2][:, :].rearrange("p (h k) -> p h k", h=H),
                                                       ALU.mult, ALU.add).then_inc(score_evac, 1)
                        dve.wait_ge(score_evac, NT * b + j + 1)
                        nc.vector.tensor_reduce(rowmax[:, j], score[:, j], AX_X, ALU.max).then_inc(max_ready, 1)
                for j in range(NT):
                    if due(b, slot, "rowsum", j):
                        dve.wait_ge(prob_ready, NT * b + j + 1)
                        own(nc.vector.tensor_reduce(rowsum[:, j], prob[:, j], AX_X, ALU.add))
                        nc.vector.reciprocal(rsum[:, j], rowsum[:, j]).then_inc(rsum_ready, 1)
                if due(b, slot, "x2"):
                    dve.wait_ge(wo_done, b + 1)
                    dve.wait_ge(xb_ready, b + 1)
                    nc.vector.tensor_tensor(x2[:, b], sc_b[:, :].rearrange("p (j d) -> p j d", j=NT), xb[:, b],
                                            ALU.add).then_inc(x2_ready, 1)
                    dve.wait_ge(x2_ready, b + 1)
                    layernorm_stats(x2[:, b], 1, stats2_ready)
                if due(b, slot, "apply2"):
                    dve.wait_ge(rstd2_ready, b + 1)
                    layernorm_apply(xn2, x2[:, b], 1, xn2_ready)
                if due(b, slot, "x2lo"):
                    dve.wait_ge(x2hi_ready, b + 1)
                    nc.vector.tensor_tensor(x2t_lo[:, b % 2], turn_a[:, :], x2t_hi[:, b % 2].bitcast(F32),
                                            ALU.subtract).then_inc(x2lo_ready, 1)
                if due(b, slot, "top"):
                    dve.wait_ge(logit_done, b + 1)
                    nc.vector.tensor_tensor(logit[:, :, :], turn_b[:, 0:NT * E].rearrange("p (j e) -> p j e", j=NT),
                                            rb_s[:, :].unsqueeze(1).broadcast_to([P, NT, E]), ALU.add).then_inc(logit_ready, 1)
                    dve.wait_ge(logit_ready, b + 1)
                    for j in range(NT):
                        last = nc.vector.max(top[:, j, :], logit[:, j, :])
                    own(last)
                    nc.vector.tensor_tensor(lead[:, :], top[:, :, 0], top[:, :, 1], ALU.subtract).then_inc(lead_ready, 1)
                    for j in range(NT):
                        last = nc.vector.max_index(topi[:, j, :], top[:, j, :], logit[:, j, :])
                    own(last)
                    for c in range(TOPK):
                        last = nc.vector.tensor_tensor(hot[:, c], cst[:, C_IOTA:C_END].unsqueeze(1).broadcast_to([P, NT, E]),
                                                       topi[:, :, c:c + 1].broadcast_to([P, NT, E]), ALU.is_equal)
                    own(last)
                if due(b, slot, "weigh"):
                    dve.wait_ge(tanh_ready, b + 1)
                    nc.vector.tensor_scalar(topw[:, :, 0], tanh[:, :], 0.5, 0.5, ALU.mult, ALU.add)
                    own(nc.vector.tensor_scalar(topw[:, :, 1], tanh[:, :], -0.5, 0.5, ALU.mult, ALU.add))
                    for c in range(TOPK):
                        last = nc.vector.tensor_tensor(hot[:, c], hot[:, c], topw[:, :, c:c + 1].broadcast_to([P, NT, E]), ALU.mult)
                    own(last)
                    own(nc.vector.tensor_tensor(comb[:, :, :], hot[:, 0], hot[:, 1], ALU.add))
                    own(nc.vector.tensor_copy(parts[:, :, 0, :], comb[:, :, :]))
                    own(nc.vector.tensor_tensor(rest1[:, :, :], comb[:, :, :], parts[:, :, 0, :], ALU.subtract))
                    own(nc.vector.tensor_copy(parts[:, :, 1, :], rest1[:, :, :]))
                    own(nc.vector.tensor_tensor(rest2[:, :, :], rest1[:, :, :], parts[:, :, 1, :], ALU.subtract))
                    nc.vector.tensor_copy(parts[:, :, 2, :], rest2[:, :, :]).then_inc(parts_ready, 1)
                if due(b, slot, "turned"):
                    dve.wait_ge(ct_done, b + 1)
                    nc.vector.tensor_copy(combt[:, :], turn_a[0:PARTS * E, 0:S // 2].bitcast(BF16)).then_inc(combt_ready, 1)

            def scale_chunk(n):
                k = n // FC
                dve.wait_ge(silu_ready, n + 1)
                dve.wait_ge(cbc_done, (k // NE) * E + k % NE)
                if n >= RING and n % FC == 1:
                    dve.wait_ge(lo1_ready, (n - RING) // FC + 1)
                nc.vector.tensor_tensor(hin[:, n % RING], silu[:, n % RING], cbc[:, :], ALU.mult).then_inc(scaled_ready, 1)

            for slot in range(SLOTS):
                k = expert_in(slot)
                if slot % 2 == 0 and 0 <= k - 1 < NK:
                    n = FC * (k - 1)
                    dve.wait_ge(hi_ready, n + 1)
                    nc.vector.tensor_tensor(hin_lo[:, n % LONG], hin[:, n % RING], hin_hi[:, n % LONG].bitcast(F32),
                                            ALU.subtract).then_inc(lo0_ready, 1)
                if slot % 2 == 1 and 0 <= k < NK and not shared(k):
                    for c in range(FC):
                        scale_chunk(FC * k + c)
                f, s = divmod(slot - UP0 - OUT_LAG - 2, SLOTS_OF_BATCH)
                if f >= 0 and s == 0 and f < B:
                    dve.wait_ge(outt_done, f + 1)
                    nc.vector.tensor_tensor(x2[:, f], sc_b[:, :].rearrange("p (j d) -> p j d", j=NT), x2[:, f],
                                            ALU.add).then_inc(res_ready, 1)
                for b in range(B):
                    attention(b, slot)
                if 6 <= slot < 6 + WCUT:
                    c = slot - 6
                    dve.wait_ge(upw_hi, c + 1)
                    nc.vector.tensor_tensor(wup_lo[:, c], wup[:, c], wup_hi[:, c].bitcast(F32), ALU.subtract).then_inc(upw_lo, 1)
                if slot == 3:
                    setup_values()
                if slot == 9:
                    setup_router()

        @block.tensor
        def _(pe):
            def split_product(dst, stationary, moving, start=True, stop=True):
                (s_hi, s_lo), (m_hi, m_lo) = stationary, moving
                nc.tensor.matmul(dst, s_hi, m_hi, start=start, stop=False)
                nc.tensor.matmul(dst, s_lo, m_hi, start=False, stop=False)
                return nc.tensor.matmul(dst, s_hi, m_lo, start=False, stop=stop)

            def weight(w, n):
                c = n % NU
                per = NU // WCUT
                return w[:, c // per, (c % per) * P:(c % per + 1) * P]

            def up(n):
                b = n // NU
                if n == 0:
                    pe.wait_ge(upw_lo, WCUT)
                if n % NU == 0:
                    pe.wait_ge(x2lo_ready, b + 1)
                if n >= FC:
                    pe.wait_ge(silu_ready, n - FC + 1)
                split_product(hid[n % FC][:, :], (weight(wup_hi, n), weight(wup_lo, n)),
                              (x2t_hi[:, b % 2], x2t_lo[:, b % 2])).then_inc(up_done, 1)

            def broadcast_weights(k):
                if k % NE == 1:
                    pe.wait_ge(combt_ready, k // NE + 1)
                before = scaled_upto(FC * k - 1)
                if before:
                    pe.wait_ge(scaled_ready, before)
                e = k % NE - 1
                nc.tensor.matmul(cbc[:, :], pick[:, e * P:(e + 1) * P], combt[:, :], start=True, stop=True).then_inc(cbc_done, 1)

            def down(n):
                c = n % NU
                if n == 0:
                    pe.wait_ge(downw_lo, WCUT)
                if c == 0 and n:
                    pe.wait_ge(yt_ready, n // NU)
                pe.wait_ge((lo0_ready, lo1_ready)[n % FC], n // FC + 1)
                split_product(yacc[:, :], (weight(wdn_hi, n), weight(wdn_lo, n)), (hin_hi[:, n % LONG], hin_lo[:, n % LONG]),
                              start=(c == 0), stop=(c == NU - 1)).then_inc(down_done, 1)

            def turn_output(f):
                pe.wait_ge(yt_ready, f + 1)
                if f + 2 < B:
                    pe.wait_ge(score_evac, NT * (f + 3))
                for j in range(NT):
                    last = nc.tensor.transpose(sc_b[:, j * P:(j + 1) * P], yt[:, j * P:(j + 1) * P], ident)
                last.then_inc(outt_done, 1)

            def attention(b, slot):
                if due(b, slot, "xt"):
                    pe.wait_ge(xn_ready, b + 1)
                    if b:
                        pe.wait_ge(pt_copied, NT * b - 1)
                    for j in range(NT):
                        last = nc.tensor.transpose(turn_a[:, j * P:(j + 1) * P], xn[:, j, :], ident)
                    last.then_inc(xt_done, 1)
                if due(b, slot, "q"):
                    if b == 0:
                        pe.wait_ge(in_wq, 32)
                    else:
                        pe.wait_ge(pt_copied, NT * b)
                    pe.wait_ge(xnt_copied, b + 1)
                    nc.tensor.matmul(turn_b[:, :], wq_s[:, :], xnt[:, :], start=True, stop=True).then_inc(q_done, 1)
                for j in range(NT):
                    if due(b, slot, "score", j):
                        if j == 0:
                            pe.wait_ge(qlo_ready, b + 1)
                            if b == 0:
                                pe.wait_ge(kblk0_ready, 1)
                            else:
                                pe.wait_ge(kblk_ready, b)
                                pe.wait_ge(ot_ready, b)
                        if j == 1 and b:
                            pe.wait_ge(x2_ready, b)
                        if j >= 2:
                            pe.wait_ge(score_evac, NT * b + j - 1)
                        t = slice(j * P, (j + 1) * P)
                        split_product((sc_a, sc_b)[j % 2][:, :], (qt_hi[:, t], qt_lo[:, t]),
                                      (kblk_hi[:, b], kblk_lo[:, b])).then_inc(s_done, 1)
                for j in range(NT):
                    if due(b, slot, "pt", j):
                        pe.wait_ge(normed_ready, NT * b + j + 1)
                        if j >= 2:
                            pe.wait_ge(pt_copied, NT * b + j - 1)
                        for g in range(NG):
                            last = nc.tensor.transpose((turn_a, turn_b)[j % 2][:, g * P:(g + 1) * P],
                                                       prob[:, j, g * GH:(g + 1) * GH].rearrange("p h k -> p (h k)"), ident)
                        last.then_inc(ptr_done, 1)
                if due(b, slot, "pv"):
                    pe.wait_ge(pt_copied, NT * (b + 1))
                    if b == 0:
                        pe.wait_ge(vblk_ready, 1)
                    for g in range(NG):
                        rows = slice(g * CTX, (g + 1) * CTX)
                        last = nc.tensor.matmul(sc_a[rows, :], vblk[:, b, rows], probt[:, g, :], start=True, stop=True)
                    last.then_inc(pv_done, 1)
                if due(b, slot, "wo"):
                    pe.wait_ge(ot_ready, b + 1)
                    if b == 0:
                        pe.wait_ge(in_wo, 16)
                    if b >= 2:
                        pe.wait_ge(res_ready, b - 1)
                    for j in range(NT):
                        last = nc.tensor.matmul(sc_b[:, j * D:(j + 1) * D], ot[:, j * P:(j + 1) * P], wo_s[:, :], start=True, stop=True)
                    last.then_inc(wo_done, 1)
                if due(b, slot, "x2t"):
                    pe.wait_ge(xn2_ready, b + 1)
                    for j in range(NT):
                        last = nc.tensor.transpose(turn_a[:, j * P:(j + 1) * P], xn2[:, j, :], ident)
                    last.then_inc(x2t_done, 1)
                if due(b, slot, "logit"):
                    pe.wait_ge(x2lo_ready, b + 1)
                    if b == 0:
                        pe.wait_ge(const_ready, 1)
                    if b + 1 < B:
                        pe.wait_ge(qlo_ready, b + 2)
                    for j in range(NT):
                        t = slice(j * P, (j + 1) * P)
                        last = split_product(turn_b[:, j * E:(j + 1) * E], (x2t_hi[:, b % 2, t], x2t_lo[:, b % 2, t]),
                                             (rt_hi[:, :], rt_lo[:, :]))
                    last.then_inc(logit_done, 1)
                if due(b, slot, "turn"):
                    pe.wait_ge(parts_ready, b + 1)
                    for j in range(NT):
                        last = nc.tensor.transpose(turn_a[0:PARTS * E, j * P // 2:(j + 1) * P // 2].bitcast(BF16),
                                                   parts[:, j].rearrange("p a e -> p (a e)"), ident16[:, :])
                    last.then_inc(ct_done, 1)

            pe.wait_ge(in_ctx, 16)
            pe.wait_ge(in_wk, 32)
            nc.tensor.matmul(hid[0][:, 0:B * CTX], wk_s[:, :], ctxt[:, :, :].rearrange("d b k -> d (b k)"),
                             start=True, stop=True).then_inc(k_done, 1)
            pe.wait_ge(in_cst, 16)
            for slot in range(SLOTS):
                k = expert_in(slot)
                if slot % 2 == 0 and 0 <= k < NK:
                    for c in range(FC):
                        up(FC * k + c)
                    if not shared(k):
                        broadcast_weights(k)
                k = (slot - UP0 - DOWN_LAG) // 2
                if slot % 2 == 1 and 0 <= k < NK:
                    for c in range(FC):
                        down(FC * k + c)
                f, s = divmod(slot - UP0 - OUT_LAG - 1, SLOTS_OF_BATCH)
                if f >= 0 and s == 0 and f < B:
                    turn_output(f)
                for b in range(B):
                    attention(b, slot)
                if slot == 2:
                    pe.wait_ge(in_wv, 16)
                    pe.wait_ge(ctxrep_ready, 1)
                    for b in range(B):
                        last = nc.tensor.matmul(yacc[:, b * D:(b + 1) * D], ctxrep[:, b].rearrange("d j k -> d (j k)"), wv_s[:, :],
                                                start=True, stop=True)
                    last.then_inc(v_done, 1)


def kernel(**inputs):
    import numpy as _np
    import concourse.bacc as _bacc
    from concourse import mybir as _mybir
    from concourse.bass_utils import run_bass_kernel_spmd as _run

    a = {k: _np.asarray(v) for k, v in inputs.items()}
    w_up = _np.concatenate([a["L0_ffn_shared_w_up"], a["L0_ffn_w_up"]])
    w_down = _np.concatenate([a["L0_ffn_shared_w_down"], a["L0_ffn_w_down"]])
    laid_out = {
        "x": a["x"],
        "ctx_t": a["ctx_1024"].transpose(2, 0, 1),
        "mask": a["mask_Bx1xSxS2_ff0"],
        "wq": a["L0_xattn_Wq"], "bq": a["L0_xattn_bq"],
        "wk": a["L0_xattn_Wk"], "bk": a["L0_xattn_bk"],
        "wv": a["L0_xattn_Wv"], "bv": a["L0_xattn_bv"],
        "wo": a["L0_xattn_Wo"], "bo": a["L0_xattn_bo"],
        "router_t": a["L0_ffn_router_w"].T, "router_b": a["L0_ffn_router_b"],
        "w_up_t": w_up.reshape(NE * F, D).T.reshape(D, WCUT, NU * P // WCUT),
        "w_down_t": w_down.reshape(NE, D, FC, P).transpose(3, 0, 2, 1).reshape(P, WCUT, NU * D // WCUT),
        "consts": shape_constants(),
        "pick_const": expert_constants(),
    }
    nc = _bacc.Bacc("TRN2", target_bir_lowering=False, num_devices=1)
    arrays, args = {}, []
    for name, value in laid_out.items():
        value = _np.ascontiguousarray(value)
        arrays[f"in_{name}"] = value
        args.append(nc.dram_tensor(f"in_{name}", value.shape, _mybir.dt.from_np(value.dtype), kind="ExternalInput").ap())
    args.append(nc.dram_tensor("out_0", (B, S, D), _mybir.dt.float32, kind="ExternalOutput").ap())
    xattn_moe(nc, *args)
    r = _run(nc, [arrays], core_ids=[0])
    return r.results[0]["out_0"]
```

```python
from contextlib import ExitStack

import numpy as np

import concourse.bass as bass
from concourse import mybir

F32 = mybir.dt.float32
F32R = mybir.dt.float32r
BF16 = mybir.dt.bfloat16
U32 = mybir.dt.uint32
ALU = mybir.AluOpType
ACT = mybir.ActivationFunctionType
AX_X = mybir.AxisListType.X

P = 128
B, S, D = 4, 512, 128
CTX = 32
H, HD = 16, 8
GH = P // CTX
NG = H // GH
NT = S // P
E, F = 8, 256
NE = E + 1
FC = F // P
NU = NE * FC
TOPK = 2
WCUT = 3
RING, LONG = 4, 6
PARTS = 3
SCALE = 1.0 / float(np.sqrt(np.float32(D)))
MASK_SCALE = -1000000000.0
LN_EPS = 1e-5

C_IDENT = 0
C_HEAD = C_IDENT + P
C_GROUP = C_HEAD + H
C_IOTA = C_GROUP + GH
C_END = C_IOTA + E

UP0 = 12
DOWN_LAG = 5
SLOTS_OF_BATCH = 2 * NE
NK = B * NE
OUT_LAG = 2 * NE + DOWN_LAG - 1
FIRST = dict(stats=0, rstd=0, apply=0, xt=0, xcopy=1, q=3, qhi=2, qlo=2, score=[3, 3, 4, 4], evac=[3, 4, 5, 6],
             shift=[3, 4, 5, 6], exp=[3, 4, 5, 6], rowsum=[5, 6, 7, 7], rsum=7, rspread=7, rturn=8, rcopy=9,
             pt=[6, 6, 7, 8], ptcopy=[4, 5, 6, 7], pv=8, ot=8, xb=7, wo=9, x2=9, rstd2=9, apply2=9, x2t=10, x2hi=11,
             x2lo=10, logit=11, top=11, tanh=11, weigh=11, turn=12, turned=13)
SECOND = dict(stats=1, rstd=1, apply=2, xt=3, xcopy=4, q=7, qhi=6, qlo=7, score=[8, 8, 8, 9], evac=[8, 8, 9, 10],
              shift=[8, 8, 9, 10], exp=[10, 11, 11, 11], rowsum=[13, 13, 13, 13], rsum=13, rspread=14, rturn=17,
              rcopy=17, pt=[15, 17, 19, 19], ptcopy=[17, 17, 18, 19], pv=20, ot=20, xb=20, wo=21, x2=22, rstd2=21,
              apply2=23, x2t=26, x2hi=25, x2lo=26, logit=30, top=30, tanh=30, weigh=31, turn=31, turned=32)
THIRD = dict(stats=-2, rstd=-1, apply=-1, xt=0, xcopy=0, q=3, qhi=3, qlo=4, score=[5, 6, 7, 7], evac=[5, 6, 7, 8],
             shift=[4, 5, 6, 7], exp=[10, 11, 11, 11], rowsum=[11, 12, 14, 14], rsum=16, rspread=16, rturn=18,
             rcopy=18, pt=[13, 16, 17, 18], ptcopy=[14, 16, 16, 17], pv=19, ot=19, xb=16, wo=21, x2=22, rstd2=20,
             apply2=23, x2t=25, x2hi=24, x2lo=25, logit=28, top=29, tanh=29, weigh=29, turn=30, turned=29)
LATER = dict(stats=-2, rstd=-4, apply=0, xt=2, xcopy=2, q=5, qhi=5, qlo=5, score=[6, 7, 8, 8], evac=[6, 7, 8, 9],
             shift=[5, 7, 8, 9], exp=[11, 11, 11, 11], rowsum=[11, 11, 13, 14], rsum=15, rspread=15, rturn=17,
             rcopy=16, pt=[13, 15, 16, 18], ptcopy=[14, 15, 17, 18], pv=20, ot=20, xb=18, wo=21, x2=22, rstd2=20,
             apply2=24, x2t=25, x2hi=25, x2lo=26, logit=27, top=27, tanh=27, weigh=27, turn=30, turned=29)
UP_HI, UP_LO = [2, 2, 9], [2, 10, 14]
DOWN_HI, DOWN_LO = [6, 8, 9], [10, 13, 15]
VALUES_PRODUCT, VALUES, ROUTER = 5, 6, 7
BLOCK_KEYS = [0, 13, 19]
OUT_COPY, OUT_TURN, OUT_ADD = OUT_LAG - 2, OUT_LAG + 2, OUT_LAG + 2
SLOTS = UP0 + SLOTS_OF_BATCH * (B - 1) + OUT_ADD + 1
BEGINS = [0, 0] + [UP0 + SLOTS_OF_BATCH * b - 28 for b in range(2, B)]


def due(b, slot, stage, j=None):
    at = (FIRST, SECOND, THIRD, LATER)[min(b, 3)][stage]
    return slot - BEGINS[b] == (at if j is None else at[j])


def tiles_due(b, slot, stage):
    tiles = [j for j in range(NT) if due(b, slot, stage, j)]
    return (tiles[0], tiles[-1] + 1) if tiles else (0, 0)


def shape_constants():
    c = np.zeros((P, C_END), np.float32)
    p = np.arange(P)
    c[:, C_IDENT:C_HEAD] = np.eye(P, dtype=np.float32)
    c[:, C_HEAD:C_GROUP] = p[:, None] // HD == np.arange(H)[None, :]
    c[:, C_GROUP:C_IOTA] = p[:, None] // CTX == np.arange(GH)[None, :]
    c[:, C_IOTA:C_END] = np.arange(E)[None, :]
    return c


def expert_constants():
    rows = np.arange(PARTS * E)
    pick = rows[:, None] % E == np.arange(E)[None, :]
    return np.repeat(pick, P, axis=1).astype(np.float32)


def xattn_moe(nc: bass.Bass, x, mask, keys_in, query_in, value_in, rows_in, w_up_t, w_down_t, pick_const, out):
    with ExitStack() as stack:
        def sb(name, shape, dt=F32):
            return stack.enter_context(nc.sbuf_tensor(name, shape, dt))

        def bank(name):
            return stack.enter_context(nc.psum_tensor(name, [P, S], F32))

        def sem(name):
            return stack.enter_context(nc.semaphore(name))

        keys_s = sb("keys_s", [D, B * CTX + D + 1])
        ctxt, wk_s, bk_s = keys_s[:, 0:B * CTX], keys_s[:, B * CTX:B * CTX + D], keys_s[:, B * CTX + D:B * CTX + D + 1]
        cst = sb("cst", [P, C_END + D + 1])
        ident = cst[:, C_IDENT:C_HEAD]
        wq_s, bq_s = cst[:, C_END:C_END + D], cst[:, C_END + D:C_END + D + 1]
        value_s = sb("value_s", [D, 2 * D + E])
        wv_s, wo_s, rt = value_s[:, 0:D], value_s[:, D:2 * D], value_s[:, 2 * D:2 * D + E]
        rows_s = sb("rows_s", [P, 2 * D + E])
        bv_s, bo_s, rb_s = rows_s[:, 0:D], rows_s[:, D:2 * D], rows_s[:, 2 * D:2 * D + E]
        pick32 = sb("pick32", [PARTS * E, E * P])
        pick = sb("pick", [PARTS * E, E * P], BF16)
        ident16 = sb("ident16", [P, P], BF16)
        xin = sb("xin", [P, B, NT, D])
        msk = sb("msk", [P, B, NT, CTX])
        ctxrep = sb("ctxrep", [D, B, GH, CTX])
        rt_hi, rt_lo = sb("rt_hi", [D, E], F32R), sb("rt_lo", [D, E], F32R)
        wup, wup_hi, wup_lo = (sb(n, [D, WCUT, NU * P // WCUT], t) for n, t in (("wup", F32), ("wup_hi", F32R), ("wup_lo", F32R)))
        wdn, wdn_hi, wdn_lo = (sb(n, [P, WCUT, NU * D // WCUT], t) for n, t in (("wdn", F32), ("wdn_hi", F32R), ("wdn_lo", F32R)))
        kt = sb("kt", [D, B, CTX])
        kt_hi, kt_lo = sb("kt_hi", [D, B, CTX], F32R), sb("kt_lo", [D, B, CTX], F32R)
        kblk_hi, kblk_lo = sb("kblk_hi", [D, B, H * CTX], F32R), sb("kblk_lo", [D, B, H * CTX], F32R)
        vrep = sb("vrep", [P, B, D])
        vblk = sb("vblk", [P, B, D])
        minus_half = sb("minus_half", [P, NT])
        stats = sb("stats", [P, NT, 6])
        mv = sb("mv", [P, 2, NT, 2])
        vareps = sb("vareps", [P, 2, NT])
        rstd = sb("rstd", [P, 2, NT])
        xn = sb("xn", [P, NT, D])
        xnt = sb("xnt", [D, S])
        qt_hi, qt_lo = sb("qt_hi", [D, S], F32R), sb("qt_lo", [D, S], F32R)
        score = sb("score", [P, NT, H, CTX])
        rowmax = sb("rowmax", [P, NT, H])
        prob = sb("prob", [P, NT, H, CTX])
        rowsum = sb("rowsum", [P, NT, H])
        rsum = sb("rsum", [P, NT, H])
        rspread = sb("rspread", [P, NT, H, HD])
        rsumt = sb("rsumt", [D, S])
        probt = sb("probt", [P, NG, S])
        ot = sb("ot", [D, S])
        xb = sb("xb", [P, B, NT, D])
        x2 = sb("x2", [P, B, NT, D])
        xn2 = sb("xn2", [P, NT, D])
        x2t_hi, x2t_lo = sb("x2t_hi", [D, 2, S], F32R), sb("x2t_lo", [D, 2, S], F32R)
        logit = sb("logit", [P, NT, E])
        top = sb("top", [P, NT, 8])
        topi = sb("topi", [P, NT, 8], U32)
        lead = sb("lead", [P, NT])
        tanh = sb("tanh", [P, NT])
        topw = sb("topw", [P, NT, TOPK])
        hot = sb("hot", [P, TOPK, NT, E])
        comb = sb("comb", [P, NT, E])
        rest1, rest2 = sb("rest1", [P, NT, E]), sb("rest2", [P, NT, E])
        parts = sb("parts", [P, NT, PARTS, E], BF16)
        combt = sb("combt", [PARTS * E, S], BF16)
        silu = sb("silu", [P, RING, S])
        hin = sb("hin", [P, RING, S])
        hin_hi, hin_lo = sb("hin_hi", [P, LONG, S], F32R), sb("hin_lo", [P, LONG, S], F32R)
        yt = sb("yt", [D, S])

        hid = [bank("hid0"), bank("hid1")]
        yacc = bank("yacc")
        cbc = bank("cbc")
        turn_a, turn_b = bank("turn_a"), bank("turn_b")
        sc_a, sc_b = bank("sc_a"), bank("sc_b")
        row_bank = [turn_a if b != 1 else hid[0] for b in range(B)]
        query_bank = [turn_b if b != 1 else hid[1] for b in range(B)]
        score_bank = [[sc_a, sc_b] * (NT // 2) if b != 1 else [hid[0], hid[1], cbc, yacc] for b in range(B)]

        in_x = [sem(f"in_x{b}") for b in range(B)]
        in_keys, in_cst, in_value, in_rows = sem("in_keys"), sem("in_cst"), sem("in_value"), sem("in_rows")
        in_mask, in_up, in_down, in_pick = sem("in_mask"), sem("in_up"), sem("in_down"), sem("in_pick")
        out_stored = sem("out_stored")
        k_done, v_done = sem("k_done"), sem("v_done")
        xt_done, q_done, s_done, ptr_done, pv_done = sem("xt_done"), sem("q_done"), sem("s_done"), sem("ptr_done"), sem("pv_done")
        rturn_done = sem("rturn_done")
        wo_done, x2t_done, logit_done, ct_done, cbc_done = sem("wo_done"), sem("x2t_done"), sem("logit_done"), sem("ct_done"), sem("cbc_done")
        up_done, down_done, outt_done = sem("up_done"), sem("down_done"), sem("outt_done")
        ctxrep_ready, upw_hi, downw_hi = sem("ctxrep_ready"), sem("upw_hi"), sem("downw_hi")
        xnt_copied, qhi_ready, prob_ready, pt_copied, rspread_ready, rsumt_ready = sem("xnt_copied"), sem("qhi_ready"), sem("prob_ready"), sem("pt_copied"), sem("rspread_ready"), sem("rsumt_ready")
        x2hi_ready, tanh_ready, silu_ready, hi_ready, yt_ready = sem("x2hi_ready"), sem("tanh_ready"), sem("silu_ready"), sem("hi_ready"), sem("yt_ready")
        dve_step = sem("dve_step")
        kt_ready, kblk0_ready, vblk_ready, const_ready, upw_lo = sem("kt_ready"), sem("kblk0_ready"), sem("vblk_ready"), sem("const_ready"), sem("upw_lo")
        stats_ready, xn_ready, qlo_ready, max_ready, rsum_ready = sem("stats_ready"), sem("xn_ready"), sem("qlo_ready"), sem("max_ready"), sem("rsum_ready")
        score_evac, rowsum_ready, ot_ready = sem("score_evac"), sem("rowsum_ready"), sem("ot_ready")
        x2_ready, stats2_ready, xn2_ready, x2lo_ready = sem("x2_ready"), sem("stats2_ready"), sem("xn2_ready"), sem("x2lo_ready")
        logit_ready, lead_ready, parts_ready, combt_ready, scaled_ready = sem("logit_ready"), sem("lead_ready"), sem("parts_ready"), sem("combt_ready"), sem("scaled_ready")
        lo0_ready, res_ready = sem("lo0_ready"), sem("res_ready")
        pool_step = sem("pool_step")
        rstd_ready, rstd2_ready, shifted_ready = sem("rstd_ready"), sem("rstd2_ready"), sem("shifted_ready")
        xb_ready, kblk_ready, downw_lo, lo1_ready = sem("xb_ready"), sem("kblk_ready"), sem("downw_lo"), sem("lo1_ready")

        def shared(k):
            return k % NE == 0

        def scaled_upto(n):
            return (n // NU) * (NU - FC) + max(0, n % NU - FC + 1)

        def expert_in(slot):
            k = (slot - UP0) // 2
            return k

        block = stack.enter_context(nc.Block())

        @block.sync
        def _(sp):
            sp.dma_start(xin[:, 0], x[0].rearrange("(p j) d -> p j d", j=NT)).then_inc(in_x[0], 16)
            sp.dma_start(cst[:, :], query_in).then_inc(in_cst, 16)
            sp.dma_start(xin[:, 1], x[1].rearrange("(p j) d -> p j d", j=NT)).then_inc(in_x[1], 16)
            sp.dma_start(wup[:, :, :], w_up_t).then_inc(in_up, 16)
            sp.dma_start(msk[:, :, :, :], mask.rearrange("b a (p j) k -> p (b a) j k", j=NT)).then_inc(in_mask, 16)
            sp.dma_start(wdn[:, :, :], w_down_t).then_inc(in_down, 16)
            sp.dma_start(pick32[:, :], pick_const).then_inc(in_pick, 16)
            for b in range(2, B):
                sp.dma_start(xin[:, b], x[b].rearrange("(p j) d -> p j d", j=NT)).then_inc(in_x[b], 16)
            for b in range(B):
                sp.wait_ge(res_ready, b + 1)
                sp.dma_start(out[b].rearrange("(p j) d -> p j d", j=NT), x2[:, b]).then_inc(out_stored, 16)
            sp.wait_ge(out_stored, 16 * B)

        @block.gpsimd
        def _(pool):
            steps = [0]

            def own(ins):
                steps[0] += 1
                ins.then_inc(pool_step, 1)
                pool.wait_ge(pool_step, steps[0])

            def root(which, b, done):
                if b:
                    pool.wait_ge(done, b)
                own(nc.gpsimd.tensor_scalar(vareps[:, which, :], mv[:, which, :, 1], LN_EPS, None, ALU.add))
                nc.gpsimd.tensor_tensor(rstd[:, which, :], vareps[:, which, :], minus_half[:, :], ALU.pow).then_inc(done, 1)

            def attention(b, slot):
                if due(b, slot, "rstd"):
                    pool.wait_ge(stats_ready, b + 1)
                    root(0, b, rstd_ready)
                lo, hi = tiles_due(b, slot, "shift")
                if hi:
                    pool.wait_ge(max_ready, NT * b + hi)
                    flat = score[:, lo:hi].rearrange("p j h k -> p (j h) k")
                    nc.gpsimd.tensor_tensor(flat, flat, rowmax[:, lo:hi].rearrange("p j h -> p (j h)").unsqueeze(2)
                                            .broadcast_to([P, (hi - lo) * H, CTX]), ALU.subtract).then_inc(shifted_ready, hi - lo)
                if due(b, slot, "xb"):
                    if b == 0:
                        pool.wait_ge(in_rows, 16)
                    pool.wait_ge(in_x[b], 16)
                    nc.gpsimd.tensor_tensor(xb[:, b], xin[:, b], bo_s[:, :].unsqueeze(1).broadcast_to([P, NT, D]),
                                            ALU.add).then_inc(xb_ready, 1)
                if due(b, slot, "rstd2"):
                    pool.wait_ge(stats2_ready, b + 1)
                    root(1, b, rstd2_ready)

            def block_keys(b):
                pool.wait_ge(kt_ready, 1)
                for part, blocks in ((kt_hi, kblk_hi), (kt_lo, kblk_lo)):
                    last = nc.gpsimd.tensor_tensor(blocks[:, b].rearrange("p (h k) -> p h k", h=H),
                                                   part[:, b].bitcast(F32).unsqueeze(1).broadcast_to([D, H, CTX]),
                                                   cst[:, C_HEAD:C_GROUP].unsqueeze(2).broadcast_to([D, H, CTX]), ALU.mult)
                last.then_inc(kblk_ready, 1)

            own(nc.gpsimd.memset(minus_half[:, :], -0.5))
            for slot in range(SLOTS):
                k = expert_in(slot) - 1
                if slot % 2 == 0 and 0 <= k < NK:
                    n = FC * k + 1
                    pool.wait_ge(hi_ready, n + 1)
                    nc.gpsimd.tensor_tensor(hin_lo[:, n % LONG], hin[:, n % RING], hin_hi[:, n % LONG].bitcast(F32),
                                            ALU.subtract).then_inc(lo1_ready, 1)
                for b in range(B):
                    attention(b, slot)
                for c in range(WCUT):
                    if slot == DOWN_LO[c]:
                        pool.wait_ge(downw_hi, c + 1)
                        nc.gpsimd.tensor_tensor(wdn_lo[:, c], wdn[:, c], wdn_hi[:, c].bitcast(F32), ALU.subtract).then_inc(downw_lo, 1)
                for b in range(1, B):
                    if slot == BLOCK_KEYS[b - 1]:
                        block_keys(b)

        @block.scalar
        def _(act):
            act.dma_start(keys_s[:, :], keys_in).then_inc(in_keys, 16)
            act.dma_start(value_s[:, :], value_in).then_inc(in_value, 16)
            act.dma_start(rows_s[:, :], rows_in.partition_broadcast(P)).then_inc(in_rows, 16)

            def silu_chunk(n):
                act.wait_ge(up_done, n + 1)
                if shared(n // FC):
                    if n >= RING:
                        act.wait_ge((lo0_ready, lo1_ready)[n % FC], (n - RING) // FC + 1)
                    nc.scalar.activation(hin[:, n % RING], hid[n % FC][:, :], ACT.Silu).then_inc(silu_ready, 1)
                else:
                    if n >= RING and scaled_upto(n - RING) > 0:
                        act.wait_ge(scaled_ready, scaled_upto(n - RING))
                    nc.scalar.activation(silu[:, n % RING], hid[n % FC][:, :], ACT.Silu).then_inc(silu_ready, 1)

            def round_chunk(n):
                if shared(n // FC):
                    act.wait_ge(silu_ready, n + 1)
                else:
                    act.wait_ge(scaled_ready, scaled_upto(n))
                if n >= LONG:
                    act.wait_ge(down_done, n - LONG + 1)
                nc.scalar.activation(hin_hi[:, n % LONG], hin[:, n % RING], ACT.Copy).then_inc(hi_ready, 1)

            def attention(b, slot):
                if due(b, slot, "xcopy"):
                    act.wait_ge(xt_done, b + 1)
                    if b:
                        act.wait_ge(q_done, b)
                    nc.scalar.activation(xnt[:, :], row_bank[b][:, :], ACT.Copy).then_inc(xnt_copied, 1)
                if due(b, slot, "qhi"):
                    act.wait_ge(q_done, b + 1)
                    if b:
                        act.wait_ge(s_done, NT * b)
                    nc.scalar.activation(qt_hi[:, :], query_bank[b][:, :], ACT.Identity, bias=bq_s[:, :]).then_inc(qhi_ready, 1)
                lo, hi = tiles_due(b, slot, "exp")
                if hi:
                    act.wait_ge(shifted_ready, NT * b + hi)
                    if b:
                        act.wait_ge(rowsum_ready, NT * (b - 1) + hi)
                        act.wait_ge(ptr_done, NT * (b - 1) + hi)
                    nc.scalar.activation(prob[:, lo:hi], score[:, lo:hi], ACT.Exp).then_inc(prob_ready, hi - lo)
                if due(b, slot, "rspread"):
                    act.wait_ge(rsum_ready, b + 1)
                    nc.scalar.activation(rspread[:, :, :, :], rsum[:, :, :].unsqueeze(3).broadcast_to([P, NT, H, HD]),
                                         ACT.Copy).then_inc(rspread_ready, 1)
                if due(b, slot, "rcopy"):
                    act.wait_ge(rturn_done, b + 1)
                    nc.scalar.activation(rsumt[:, :], sc_b[:, :], ACT.Copy).then_inc(rsumt_ready, 1)
                for j in range(NT):
                    if due(b, slot, "ptcopy", j):
                        act.wait_ge(ptr_done, NT * b + j + 1)
                        nc.scalar.activation(probt[:, :, j * P:(j + 1) * P],
                                             (turn_a, turn_b)[j % 2][:, :].rearrange("p (g t) -> p g t", g=NG),
                                             ACT.Copy).then_inc(pt_copied, 1)
                if due(b, slot, "x2hi"):
                    act.wait_ge(x2t_done, b + 1)
                    nc.scalar.activation(x2t_hi[:, b % 2], turn_a[:, :], ACT.Copy).then_inc(x2hi_ready, 1)
                if due(b, slot, "tanh"):
                    act.wait_ge(lead_ready, b + 1)
                    nc.scalar.activation(tanh[:, :], lead[:, :], ACT.Tanh, scale=0.5).then_inc(tanh_ready, 1)

            act.wait_ge(in_keys, 16)
            nc.scalar.activation(ctxrep[:, :, :, :], ctxt.rearrange("d (b k) -> d b k", b=B).unsqueeze(2).broadcast_to([D, B, GH, CTX]),
                                 ACT.Copy).then_inc(ctxrep_ready, 1)
            for slot in range(SLOTS):
                k = expert_in(slot)
                if 0 <= k < NK:
                    for c in range(FC):
                        (silu_chunk, round_chunk)[slot % 2](FC * k + c)
                f, s = divmod(slot - UP0 - OUT_COPY, SLOTS_OF_BATCH)
                if f >= 0 and s == 0 and f < B:
                    act.wait_ge(down_done, NU * (f + 1))
                    nc.scalar.activation(yt[:, :], yacc[:, :], ACT.Copy).then_inc(yt_ready, 1)
                for b in range(B):
                    attention(b, slot)
                for c in range(WCUT):
                    if slot == UP_HI[c]:
                        act.wait_ge(in_up, 16)
                        nc.scalar.activation(wup_hi[:, c], wup[:, c], ACT.Copy).then_inc(upw_hi, 1)
                for c in range(WCUT):
                    if slot == DOWN_HI[c]:
                        act.wait_ge(in_down, 16)
                        nc.scalar.activation(wdn_hi[:, c], wdn[:, c], ACT.Copy).then_inc(downw_hi, 1)

        @block.vector
        def _(dve):
            steps = [0]

            def own(ins):
                steps[0] += 1
                ins.then_inc(dve_step, 1)
                dve.wait_ge(dve_step, steps[0])

            def layernorm_stats(src, which, done):
                for j in range(NT):
                    last = nc.vector.bn_stats(stats[:, j, :], src[:, j, :])
                own(last)
                for j in range(NT):
                    last = nc.vector.bn_aggr(mv[:, which, j, :], stats[:, j, :])
                last.then_inc(done, 1)

            def layernorm_apply(dst, src, which, done):
                for j in range(NT):
                    nc.vector.tensor_scalar(dst[:, j, :], src[:, j, :], mv[:, which, j, 0:1], rstd[:, which, j:j + 1],
                                            ALU.subtract, ALU.mult).then_inc(done, 1)

            def setup_keys():
                dve.wait_ge(in_cst, 16)
                dve.wait_ge(k_done, 1)
                own(nc.vector.tensor_scalar(kt[:, :, :].rearrange("p b k -> p (b k)"), hid[0][:, 0:B * CTX], bk_s[:, :], SCALE,
                                            ALU.add, ALU.mult))
                own(nc.vector.tensor_copy(kt_hi[:, :, :], kt[:, :, :]))
                nc.vector.tensor_tensor(kt_lo[:, :, :], kt[:, :, :], kt_hi[:, :, :].bitcast(F32), ALU.subtract).then_inc(kt_ready, 1)

            def first_blocks():
                dve.wait_ge(kt_ready, 1)
                for part, blocks in ((kt_hi, kblk_hi), (kt_lo, kblk_lo)):
                    last = nc.vector.tensor_tensor(blocks[:, 0].rearrange("p (h k) -> p h k", h=H),
                                                   part[:, 0].bitcast(F32).unsqueeze(1).broadcast_to([D, H, CTX]),
                                                   cst[:, C_HEAD:C_GROUP].unsqueeze(2).broadcast_to([D, H, CTX]), ALU.mult)
                last.then_inc(kblk0_ready, 1)

            def setup_values():
                dve.wait_ge(v_done, 1)
                dve.wait_ge(in_rows, 16)
                own(nc.vector.tensor_tensor(vrep[:, :, :], yacc[:, :].rearrange("p (b d) -> p b d", b=B),
                                            bv_s[:, :].unsqueeze(1).broadcast_to([P, B, D]), ALU.add))
                groups = cst[:, C_GROUP:C_IOTA].unsqueeze(1).unsqueeze(3).broadcast_to([P, B * NG, GH, HD])
                nc.vector.tensor_tensor(vblk[:, :, :].rearrange("p b (g j d) -> p (b g) j d", g=NG, j=GH),
                                        vrep[:, :, :].rearrange("p b (g j d) -> p (b g) j d", g=NG, j=GH),
                                        groups, ALU.mult).then_inc(vblk_ready, 1)

            def setup_router():
                dve.wait_ge(in_pick, 16)
                nc.vector.tensor_copy(pick[:, :], pick32[:, :])
                nc.vector.tensor_copy(ident16[:, :], ident)
                dve.wait_ge(in_value, 16)
                own(nc.vector.tensor_copy(rt_hi[:, :], rt[:, :]))
                nc.vector.tensor_tensor(rt_lo[:, :], rt[:, :], rt_hi[:, :].bitcast(F32), ALU.subtract).then_inc(const_ready, 1)

            def attention(b, slot):
                if due(b, slot, "stats"):
                    dve.wait_ge(in_x[b], 16)
                    layernorm_stats(xin[:, b], 0, stats_ready)
                    if b == 0:
                        setup_keys()
                if due(b, slot, "apply"):
                    dve.wait_ge(rstd_ready, b + 1)
                    if b:
                        dve.wait_ge(xt_done, b)
                    layernorm_apply(xn, xin[:, b], 0, xn_ready)
                    if b == 0:
                        first_blocks()
                if due(b, slot, "qlo"):
                    dve.wait_ge(qhi_ready, b + 1)
                    nc.vector.scalar_tensor_tensor(qt_lo[:, :], query_bank[b][:, :], bq_s[:, :], qt_hi[:, :].bitcast(F32),
                                                   ALU.add, ALU.subtract).then_inc(qlo_ready, 1)
                for j in range(NT):
                    if due(b, slot, "evac", j):
                        if j == 0 and b == 0:
                            dve.wait_ge(in_mask, 16)
                        dve.wait_ge(s_done, NT * b + j + 1)
                        nc.vector.scalar_tensor_tensor(score[:, j], msk[:, b, j].unsqueeze(1).broadcast_to([P, H, CTX]), MASK_SCALE,
                                                       score_bank[b][j][:, :].rearrange("p (h k) -> p h k", h=H),
                                                       ALU.mult, ALU.add).then_inc(score_evac, 1)
                        dve.wait_ge(score_evac, NT * b + j + 1)
                        nc.vector.tensor_reduce(rowmax[:, j], score[:, j], AX_X, ALU.max).then_inc(max_ready, 1)
                lo, hi = tiles_due(b, slot, "rowsum")
                if hi:
                    dve.wait_ge(prob_ready, NT * b + hi)
                    nc.vector.tensor_reduce(rowsum[:, lo:hi], prob[:, lo:hi], AX_X, ALU.add).then_inc(rowsum_ready, hi - lo)
                if due(b, slot, "rsum"):
                    dve.wait_ge(rowsum_ready, NT * (b + 1))
                    nc.vector.reciprocal(rsum[:, :, :], rowsum[:, :, :]).then_inc(rsum_ready, 1)
                if due(b, slot, "ot"):
                    dve.wait_ge(pv_done, b + 1)
                    dve.wait_ge(rsumt_ready, b + 1)
                    nc.vector.tensor_tensor(ot[:, :], sc_a[:, :], rsumt[:, :], ALU.mult).then_inc(ot_ready, 1)
                if due(b, slot, "x2"):
                    dve.wait_ge(wo_done, b + 1)
                    dve.wait_ge(xb_ready, b + 1)
                    nc.vector.tensor_tensor(x2[:, b], sc_b[:, :].rearrange("p (j d) -> p j d", j=NT), xb[:, b],
                                            ALU.add).then_inc(x2_ready, 1)
                    dve.wait_ge(x2_ready, b + 1)
                    layernorm_stats(x2[:, b], 1, stats2_ready)
                if due(b, slot, "apply2"):
                    dve.wait_ge(rstd2_ready, b + 1)
                    layernorm_apply(xn2, x2[:, b], 1, xn2_ready)
                if due(b, slot, "x2lo"):
                    dve.wait_ge(x2hi_ready, b + 1)
                    nc.vector.tensor_tensor(x2t_lo[:, b % 2], turn_a[:, :], x2t_hi[:, b % 2].bitcast(F32),
                                            ALU.subtract).then_inc(x2lo_ready, 1)
                if due(b, slot, "top"):
                    dve.wait_ge(logit_done, b + 1)
                    nc.vector.tensor_tensor(logit[:, :, :], turn_b[:, 0:NT * E].rearrange("p (j e) -> p j e", j=NT),
                                            rb_s[:, :].unsqueeze(1).broadcast_to([P, NT, E]), ALU.add).then_inc(logit_ready, 1)
                    dve.wait_ge(logit_ready, b + 1)
                    for j in range(NT):
                        last = nc.vector.max(top[:, j, :], logit[:, j, :])
                    own(last)
                    nc.vector.tensor_tensor(lead[:, :], top[:, :, 0], top[:, :, 1], ALU.subtract).then_inc(lead_ready, 1)
                    for j in range(NT):
                        last = nc.vector.max_index(topi[:, j, :], top[:, j, :], logit[:, j, :])
                    own(last)
                    for c in range(TOPK):
                        last = nc.vector.tensor_tensor(hot[:, c], cst[:, C_IOTA:C_END].unsqueeze(1).broadcast_to([P, NT, E]),
                                                       topi[:, :, c:c + 1].broadcast_to([P, NT, E]), ALU.is_equal)
                    own(last)
                if due(b, slot, "weigh"):
                    dve.wait_ge(tanh_ready, b + 1)
                    nc.vector.tensor_scalar(topw[:, :, 0], tanh[:, :], 0.5, 0.5, ALU.mult, ALU.add)
                    own(nc.vector.tensor_scalar(topw[:, :, 1], tanh[:, :], -0.5, 0.5, ALU.mult, ALU.add))
                    for c in range(TOPK):
                        last = nc.vector.tensor_tensor(hot[:, c], hot[:, c], topw[:, :, c:c + 1].broadcast_to([P, NT, E]), ALU.mult)
                    own(last)
                    own(nc.vector.tensor_tensor(comb[:, :, :], hot[:, 0], hot[:, 1], ALU.add))
                    own(nc.vector.tensor_copy(parts[:, :, 0, :], comb[:, :, :]))
                    own(nc.vector.tensor_tensor(rest1[:, :, :], comb[:, :, :], parts[:, :, 0, :], ALU.subtract))
                    own(nc.vector.tensor_copy(parts[:, :, 1, :], rest1[:, :, :]))
                    own(nc.vector.tensor_tensor(rest2[:, :, :], rest1[:, :, :], parts[:, :, 1, :], ALU.subtract))
                    nc.vector.tensor_copy(parts[:, :, 2, :], rest2[:, :, :]).then_inc(parts_ready, 1)
                if due(b, slot, "turned"):
                    dve.wait_ge(ct_done, b + 1)
                    nc.vector.tensor_copy(combt[:, :], turn_a[0:PARTS * E, 0:S // 2].bitcast(BF16)).then_inc(combt_ready, 1)

            def scale_chunk(n):
                k = n // FC
                dve.wait_ge(silu_ready, n + 1)
                dve.wait_ge(cbc_done, (k // NE) * E + k % NE)
                if n >= RING and n % FC == 1:
                    dve.wait_ge(lo1_ready, (n - RING) // FC + 1)
                nc.vector.tensor_tensor(hin[:, n % RING], silu[:, n % RING], cbc[:, :], ALU.mult).then_inc(scaled_ready, 1)

            for slot in range(SLOTS):
                k = expert_in(slot)
                if slot % 2 == 0 and 0 <= k - 1 < NK:
                    n = FC * (k - 1)
                    dve.wait_ge(hi_ready, n + 1)
                    nc.vector.tensor_tensor(hin_lo[:, n % LONG], hin[:, n % RING], hin_hi[:, n % LONG].bitcast(F32),
                                            ALU.subtract).then_inc(lo0_ready, 1)
                if slot % 2 == 1 and 0 <= k < NK and not shared(k):
                    for c in range(FC):
                        scale_chunk(FC * k + c)
                f, s = divmod(slot - UP0 - OUT_ADD, SLOTS_OF_BATCH)
                if f >= 0 and s == 0 and f < B:
                    dve.wait_ge(outt_done, f + 1)
                    nc.vector.tensor_tensor(x2[:, f], sc_b[:, :].rearrange("p (j d) -> p j d", j=NT), x2[:, f],
                                            ALU.add).then_inc(res_ready, 1)
                for b in range(B):
                    attention(b, slot)
                for c in range(WCUT):
                    if slot == UP_LO[c]:
                        dve.wait_ge(upw_hi, c + 1)
                        nc.vector.tensor_tensor(wup_lo[:, c], wup[:, c], wup_hi[:, c].bitcast(F32), ALU.subtract).then_inc(upw_lo, 1)
                if slot == VALUES:
                    setup_values()
                if slot == ROUTER:
                    setup_router()

        @block.tensor
        def _(pe):
            def split_product(dst, stationary, moving, start=True, stop=True, low=None):
                (s_hi, s_lo), (m_hi, m_lo) = stationary, moving
                nc.tensor.matmul(dst, s_hi, m_hi, start=start, stop=False)
                nc.tensor.matmul(dst, s_lo, m_hi, start=False, stop=False)
                if low is not None:
                    pe.wait_ge(*low)
                return nc.tensor.matmul(dst, s_hi, m_lo, start=False, stop=stop)

            def weight(w, n):
                c = n % NU
                per = NU // WCUT
                return w[:, c // per, (c % per) * P:(c % per + 1) * P]

            def up(n):
                b = n // NU
                if b == 0 and n % (NU // WCUT) == 0:
                    pe.wait_ge(upw_lo, n // (NU // WCUT) + 1)
                if n % NU == 0:
                    pe.wait_ge(x2hi_ready, b + 1)
                if n < FC:
                    pe.wait_ge(score_evac, NT + n + 1)
                else:
                    pe.wait_ge(silu_ready, n - FC + 1)
                split_product(hid[n % FC][:, :], (weight(wup_hi, n), weight(wup_lo, n)),
                              (x2t_hi[:, b % 2], x2t_lo[:, b % 2]),
                              low=(x2lo_ready, b + 1) if n % NU == 0 else None).then_inc(up_done, 1)

            def broadcast_weights(k):
                if k % NE == 1:
                    pe.wait_ge(combt_ready, k // NE + 1)
                if k == 1:
                    pe.wait_ge(score_evac, NT + 3)
                before = scaled_upto(FC * k - 1)
                if before:
                    pe.wait_ge(scaled_ready, before)
                e = k % NE - 1
                nc.tensor.matmul(cbc[:, :], pick[:, e * P:(e + 1) * P], combt[:, :], start=True, stop=True).then_inc(cbc_done, 1)

            def down(n):
                c = n % NU
                if n < NU and n % (NU // WCUT) == 0:
                    pe.wait_ge(downw_lo, n // (NU // WCUT) + 1)
                if n == 0:
                    pe.wait_ge(score_evac, 2 * NT)
                elif c == 0:
                    pe.wait_ge(yt_ready, n // NU)
                pe.wait_ge(hi_ready, n + 1)
                split_product(yacc[:, :], (weight(wdn_hi, n), weight(wdn_lo, n)), (hin_hi[:, n % LONG], hin_lo[:, n % LONG]),
                              start=(c == 0), stop=(c == NU - 1),
                              low=((lo0_ready, lo1_ready)[n % FC], n // FC + 1)).then_inc(down_done, 1)

            def turn_output(f):
                pe.wait_ge(yt_ready, f + 1)
                if f + 2 < B:
                    pe.wait_ge(score_evac, NT * (f + 3))
                for j in range(NT):
                    last = nc.tensor.transpose(sc_b[:, j * P:(j + 1) * P], yt[:, j * P:(j + 1) * P], ident)
                last.then_inc(outt_done, 1)

            def attention(b, slot):
                if due(b, slot, "xt"):
                    if b == 1:
                        pe.wait_ge(kt_ready, 1)
                    if b >= 2:
                        pe.wait_ge(pt_copied, NT * b - 1)
                    for j in range(NT):
                        pe.wait_ge(xn_ready, NT * b + j + 1)
                        last = nc.tensor.transpose(row_bank[b][:, j * P:(j + 1) * P], xn[:, j, :], ident)
                    last.then_inc(xt_done, 1)
                if due(b, slot, "q"):
                    if b >= 2:
                        pe.wait_ge(pt_copied, NT * b)
                    pe.wait_ge(xnt_copied, b + 1)
                    nc.tensor.matmul(query_bank[b][:, :], wq_s[:, :], xnt[:, :], start=True, stop=True).then_inc(q_done, 1)
                for j in range(NT):
                    if due(b, slot, "score", j):
                        if j == 0:
                            pe.wait_ge(qlo_ready, b + 1)
                            if b == 0:
                                pe.wait_ge(kblk0_ready, 1)
                            else:
                                pe.wait_ge(kblk_ready, b)
                            if b >= 2:
                                pe.wait_ge(ot_ready, b)
                        if b == 1 and j == 0:
                            pe.wait_ge(xnt_copied, 2)
                        if b == 1 and j == 3:
                            pe.wait_ge(vblk_ready, 1)
                        if b >= 2 and j == 1:
                            pe.wait_ge(x2_ready, b)
                        if b != 1 and j >= 2:
                            pe.wait_ge(score_evac, NT * b + j - 1)
                        t = slice(j * P, (j + 1) * P)
                        split_product(score_bank[b][j][:, :], (qt_hi[:, t], qt_lo[:, t]),
                                      (kblk_hi[:, b], kblk_lo[:, b])).then_inc(s_done, 1)
                for j in range(NT):
                    if due(b, slot, "pt", j):
                        pe.wait_ge(prob_ready, NT * b + j + 1)
                        if j == 0 and b:
                            pe.wait_ge(combt_ready, b)
                        if j >= 2:
                            pe.wait_ge(pt_copied, NT * b + j - 1)
                        for g in range(NG):
                            last = nc.tensor.transpose((turn_a, turn_b)[j % 2][:, g * P:(g + 1) * P],
                                                       prob[:, j, g * GH:(g + 1) * GH].rearrange("p h k -> p (h k)"), ident)
                        last.then_inc(ptr_done, 1)
                if due(b, slot, "rturn"):
                    pe.wait_ge(rspread_ready, b + 1)
                    if b >= 2:
                        pe.wait_ge(res_ready, b - 1)
                    for j in range(NT):
                        last = nc.tensor.transpose(sc_b[:, j * P:(j + 1) * P], rspread[:, j].rearrange("p h d -> p (h d)"), ident)
                    last.then_inc(rturn_done, 1)
                if due(b, slot, "pv"):
                    pe.wait_ge(pt_copied, NT * (b + 1))
                    if b == 0:
                        pe.wait_ge(vblk_ready, 1)
                    for g in range(NG):
                        rows = slice(g * CTX, (g + 1) * CTX)
                        last = nc.tensor.matmul(sc_a[rows, :], vblk[:, b, rows], probt[:, g, :], start=True, stop=True)
                    last.then_inc(pv_done, 1)
                if due(b, slot, "wo"):
                    pe.wait_ge(ot_ready, b + 1)
                    for j in range(NT):
                        last = nc.tensor.matmul(sc_b[:, j * D:(j + 1) * D], ot[:, j * P:(j + 1) * P], wo_s[:, :], start=True, stop=True)
                    last.then_inc(wo_done, 1)
                if due(b, slot, "x2t"):
                    if 0 < b < B - 1:
                        pe.wait_ge(xnt_copied, b + 2)
                    for j in range(NT):
                        pe.wait_ge(xn2_ready, NT * b + j + 1)
                        last = nc.tensor.transpose(turn_a[:, j * P:(j + 1) * P], xn2[:, j, :], ident)
                    last.then_inc(x2t_done, 1)
                if due(b, slot, "logit"):
                    pe.wait_ge(x2lo_ready, b + 1)
                    if b == 0:
                        pe.wait_ge(const_ready, 1)
                    if 0 < b < B - 1:
                        pe.wait_ge(qlo_ready, b + 2)
                    for j in range(NT):
                        t = slice(j * P, (j + 1) * P)
                        last = split_product(turn_b[:, j * E:(j + 1) * E], (x2t_hi[:, b % 2, t], x2t_lo[:, b % 2, t]),
                                             (rt_hi[:, :], rt_lo[:, :]))
                    last.then_inc(logit_done, 1)
                if due(b, slot, "turn"):
                    pe.wait_ge(parts_ready, b + 1)
                    for j in range(NT):
                        last = nc.tensor.transpose(turn_a[0:PARTS * E, j * P // 2:(j + 1) * P // 2].bitcast(BF16),
                                                   parts[:, j].rearrange("p a e -> p (a e)"), ident16[:, :])
                    last.then_inc(ct_done, 1)

            pe.wait_ge(in_keys, 16)
            nc.tensor.matmul(hid[0][:, 0:B * CTX], wk_s[:, :], ctxt[:, :],
                             start=True, stop=True).then_inc(k_done, 1)
            pe.wait_ge(in_cst, 16)
            for slot in range(SLOTS):
                k = expert_in(slot)
                if slot % 2 == 0 and 0 <= k < NK:
                    for c in range(FC):
                        up(FC * k + c)
                if slot % 2 == 1 and 0 <= k < NK and not shared(k):
                    broadcast_weights(k)
                k = (slot - UP0 - DOWN_LAG) // 2
                if slot % 2 == 1 and 0 <= k < NK:
                    for c in range(FC):
                        down(FC * k + c)
                f, s = divmod(slot - UP0 - OUT_TURN, SLOTS_OF_BATCH)
                if f >= 0 and s == 0 and f < B:
                    turn_output(f)
                for b in range(B):
                    attention(b, slot)
                if slot == VALUES_PRODUCT:
                    pe.wait_ge(in_value, 16)
                    pe.wait_ge(ctxrep_ready, 1)
                    for b in range(B):
                        last = nc.tensor.matmul(yacc[:, b * D:(b + 1) * D], ctxrep[:, b].rearrange("d j k -> d (j k)"), wv_s[:, :],
                                                start=True, stop=True)
                    last.then_inc(v_done, 1)


def kernel(**inputs):
    import numpy as _np
    import concourse.bacc as _bacc
    from concourse import mybir as _mybir
    from concourse.bass_utils import run_bass_kernel_spmd as _run

    a = {k: _np.asarray(v) for k, v in inputs.items()}
    w_up = _np.concatenate([a["L0_ffn_shared_w_up"], a["L0_ffn_w_up"]])
    w_down = _np.concatenate([a["L0_ffn_shared_w_down"], a["L0_ffn_w_down"]])
    laid_out = {
        "x": a["x"],
        "mask": a["mask_Bx1xSxS2_ff0"],
        "keys_in": _np.concatenate([a["ctx_1024"].reshape(B * CTX, D).T, a["L0_xattn_Wk"], a["L0_xattn_bk"][:, None]], axis=1),
        "query_in": _np.concatenate([shape_constants(), a["L0_xattn_Wq"], a["L0_xattn_bq"][:, None]], axis=1),
        "value_in": _np.concatenate([a["L0_xattn_Wv"], a["L0_xattn_Wo"], a["L0_ffn_router_w"].T], axis=1),
        "rows_in": _np.concatenate([a["L0_xattn_bv"], a["L0_xattn_bo"], a["L0_ffn_router_b"]]),
        "w_up_t": w_up.reshape(NE * F, D).T.reshape(D, WCUT, NU * P // WCUT),
        "w_down_t": w_down.reshape(NE, D, FC, P).transpose(3, 0, 2, 1).reshape(P, WCUT, NU * D // WCUT),
        "pick_const": expert_constants(),
    }
    nc = _bacc.Bacc("TRN2", target_bir_lowering=False, num_devices=1)
    arrays, args = {}, []
    for name, value in laid_out.items():
        value = _np.ascontiguousarray(value)
        arrays[f"in_{name}"] = value
        args.append(nc.dram_tensor(f"in_{name}", value.shape, _mybir.dt.from_np(value.dtype), kind="ExternalInput").ap())
    args.append(nc.dram_tensor("out_0", (B, S, D), _mybir.dt.float32, kind="ExternalOutput").ap())
    xattn_moe(nc, *args)
    r = _run(nc, [arrays], core_ids=[0])
    return r.results[0]["out_0"]
```
